# Optimizing a Trainium2 kernel written in Bass

```python
import numpy as np
import jax
import jax.numpy as jnp

def _softmax(x, axis=-1):
    return jax.nn.softmax(x, axis=axis)

def _gelu(x):
    return jax.nn.gelu(x, approximate=True)

def _silu(x):
    return jax.nn.silu(x)

def _sigmoid(x):
    return jax.nn.sigmoid(x)

def _layernorm(x, axis=-1, eps=1e-05):
    m = jnp.mean(x, axis=axis, keepdims=True)
    v = jnp.var(x, axis=axis, keepdims=True)
    return (x - m) / jnp.sqrt(v + eps)

def _scatter_add(tgt, idx, src, axis=0):
    return tgt.at[idx].add(src)

def _segment_sum(src, seg, n):
    return jax.ops.segment_sum(src, seg, n)
kernel_name = 'mk_xattn_ffn_d1_seqx_r4_575066'

def setup_inputs(seed: int=0):
    np.random.seed(seed)
    _w = jnp.asarray

    def _rec_inputs():
        import jax
        import jax.numpy as jnp
        _rk = jax.random.key(seed)
        x = 7.22e-05 + 1 * jax.random.normal(jax.random.fold_in(_rk, 1), (4, 1024, 256), jnp.float32)
        _lenS = 1024 - jax.random.randint(jax.random.fold_in(_rk, 7), (4,), 0, max(1, 1024 // 4) + 1, jnp.int32)
        _lenS2 = 64 - jax.random.randint(jax.random.fold_in(_rk, 8), (4,), 0, max(1, 64 // 4) + 1, jnp.int32)
        _ctx_768P = jax.random.normal(jax.random.fold_in(_rk, 11), (4, 16, 192), jnp.float32)
        _ctx_768c = jax.random.dirichlet(jax.random.fold_in(_rk, 511), 0.3 * jnp.ones((16,), jnp.float32), (4, 64))
        _ctx_768t = jnp.einsum('bsk,bkd->bsd', _ctx_768c, _ctx_768P)
        _ctx_768t = _ctx_768t * jax.lax.rsqrt(jnp.mean(jnp.square(_ctx_768t)) + 1e-12) * 0.953939
        ctx_768 = -0.000191848 + 0.999787 * (_ctx_768t + 0.3 * jax.random.normal(jax.random.fold_in(_rk, 611), (4, 64, 192), jnp.float32))
        return (x, ctx_768)
    x, ctx_768 = _rec_inputs()

    def _L0_xattn_setup():
        import jax, jax.numpy as jnp
        import numpy as np
        NUM_HEADS = 16
        CLAMP = 10000.0
        key = jax.random.key(seed)
        ks = jax.random.split(key, 8)
        B, Nq, Nkv, Cq, Ckv = (4, 512, 512, 256, 192)
        s_q = 1.0 / np.sqrt(Cq)
        s_kv = 1.0 / np.sqrt(Ckv)
        return {'query': jax.random.normal(ks[0], (B, Nq, Cq), jnp.float32), 'key_value': jax.random.normal(ks[1], (B, Nkv, Ckv), jnp.float32), 'Wq': jax.random.normal(ks[2], (Cq, Cq), jnp.float32) * s_q, 'bq': jnp.zeros((Cq,), jnp.float32), 'Wk': jax.random.normal(ks[3], (Ckv, Cq), jnp.float32) * s_kv, 'bk': jnp.zeros((Cq,), jnp.float32), 'Wv': jax.random.normal(ks[4], (Ckv, Cq), jnp.float32) * s_kv, 'bv': jnp.zeros((Cq,), jnp.float32), 'Wo': jax.random.normal(ks[5], (Cq, Cq), jnp.float32) * s_q, 'bo': jnp.zeros((Cq,), jnp.float32)}
    _L0_xattn_all = _L0_xattn_setup()
    _L0_xattn_in = {k: v for k, v in _L0_xattn_all.items() if k in ('Wq', 'bq', 'Wk', 'bk', 'Wv', 'bv', 'Wo', 'bo')}
    del _L0_xattn_all

    def _L0_ffn_setup():
        import jax, jax.numpy as jnp
        import numpy as np
        E = 8
        TOP_K = 2
        SCALE = 1.0

        def _swiglu(x, wg, wu, wd):
            gate = jax.nn.silu(x @ wg.T)
            up = x @ wu.T
            return gate * up @ wd.T
        key = jax.random.key(seed)
        ks = jax.random.split(key, 8)
        B, L, D, H = (2, 512, 256, 512)
        s = 0.02
        return {'x': jax.random.normal(ks[0], (B, L, D), jnp.float32), 'gate_w': jax.random.normal(ks[1], (E, D), jnp.float32) * s, 'sh_gate': jax.random.normal(ks[2], (H, D), jnp.float32) * s, 'sh_up': jax.random.normal(ks[3], (H, D), jnp.float32) * s, 'sh_down': jax.random.normal(ks[4], (D, H), jnp.float32) * s, 'eg': jax.random.normal(ks[5], (E, H, D), jnp.float32) * s, 'eu': jax.random.normal(ks[6], (E, H, D), jnp.float32) * s, 'ed': jax.random.normal(ks[7], (E, D, H), jnp.float32) * s}
    _L0_ffn_all = _L0_ffn_setup()
    _L0_ffn_in = {k: v for k, v in _L0_ffn_all.items() if k in ('gate_w', 'sh_gate', 'sh_up', 'sh_down', 'eg', 'eu', 'ed')}
    del _L0_ffn_all
    return {'x': x, 'ctx_768': ctx_768, 'L0_xattn_Wq': _L0_xattn_in['Wq'], 'L0_xattn_bq': _L0_xattn_in['bq'], 'L0_xattn_Wk': _L0_xattn_in['Wk'], 'L0_xattn_bk': _L0_xattn_in['bk'], 'L0_xattn_Wv': _L0_xattn_in['Wv'], 'L0_xattn_bv': _L0_xattn_in['bv'], 'L0_xattn_Wo': _L0_xattn_in['Wo'], 'L0_xattn_bo': _L0_xattn_in['bo'], 'L0_ffn_gate_w': _L0_ffn_in['gate_w'], 'L0_ffn_sh_gate': _L0_ffn_in['sh_gate'], 'L0_ffn_sh_up': _L0_ffn_in['sh_up'], 'L0_ffn_sh_down': _L0_ffn_in['sh_down'], 'L0_ffn_eg': _L0_ffn_in['eg'], 'L0_ffn_eu': _L0_ffn_in['eu'], 'L0_ffn_ed': _L0_ffn_in['ed']}

def reference(x, ctx_768, L0_xattn_Wq, L0_xattn_bq, L0_xattn_Wk, L0_xattn_bk, L0_xattn_Wv, L0_xattn_bv, L0_xattn_Wo, L0_xattn_bo, L0_ffn_gate_w, L0_ffn_sh_gate, L0_ffn_sh_up, L0_ffn_sh_down, L0_ffn_eg, L0_ffn_eu, L0_ffn_ed):
    import jax
    import jax.numpy as jnp

    def _L0_xattn_ref(query, key_value, Wq, bq, Wk, bk, Wv, bv, Wo, bo):
        import jax, jax.numpy as jnp
        import numpy as np
        NUM_HEADS = 16
        CLAMP = 10000.0
        B, Nq, Cq = query.shape
        Nkv = key_value.shape[1]
        H = NUM_HEADS
        D = Cq // H
        scale = D ** (-0.5)
        q = (query @ Wq + bq).reshape(B, Nq, H, D).transpose(0, 2, 1, 3)
        k = (key_value @ Wk + bk).reshape(B, Nkv, H, D).transpose(0, 2, 1, 3)
        v = (key_value @ Wv + bv).reshape(B, Nkv, H, D).transpose(0, 2, 1, 3)
        attn = jnp.einsum('bhqd,bhkd->bhqk', q, k) * scale
        attn = jnp.clip(attn, -CLAMP, CLAMP)
        attn = jax.nn.softmax(attn, axis=-1)
        attn = jnp.where(jnp.any(jnp.isnan(attn)), jnp.asarray(1.0 / Nkv, attn.dtype), attn)
        x = jnp.einsum('bhqk,bhkd->bqhd', attn, v).reshape(B, Nq, Cq)
        return x @ Wo + bo

    def _L0_ffn_ref(x, gate_w, sh_gate, sh_up, sh_down, eg, eu, ed):
        import jax, jax.numpy as jnp
        import numpy as np
        E = 8
        TOP_K = 2
        SCALE = 1.0

        def _swiglu(x, wg, wu, wd):
            gate = jax.nn.silu(x @ wg.T)
            up = x @ wu.T
            return gate * up @ wd.T
        B, L, D = x.shape
        T = B * L
        xf = x.reshape(T, D)
        shared = _swiglu(xf, sh_gate, sh_up, sh_down)
        router_logits = xf @ gate_w.T
        router_probs = jax.nn.softmax(router_logits.astype(jnp.float32), axis=-1)
        w, idx = jax.lax.top_k(router_probs, TOP_K)
        w = w / jnp.sum(w, axis=-1, keepdims=True)
        w = w.astype(x.dtype)
        comb = jnp.zeros((T, E), dtype=x.dtype).at[jnp.arange(T)[:, None], idx].add(w)
        g = jax.nn.silu(jnp.einsum('td,ehd->teh', xf, eg))
        u = jnp.einsum('td,ehd->teh', xf, eu)
        eo = jnp.einsum('teh,edh->ted', g * u, ed)
        routed = jnp.einsum('ted,te->td', eo, comb)
        out = shared + SCALE * routed
        return out.reshape(B, L, D)
    x = x + _L0_xattn_ref(_layernorm(x, axis=-1), ctx_768, L0_xattn_Wq, L0_xattn_bq, L0_xattn_Wk, L0_xattn_bk, L0_xattn_Wv, L0_xattn_bv, L0_xattn_Wo, L0_xattn_bo)
    x = x + _L0_ffn_ref(_layernorm(x, axis=-1), L0_ffn_gate_w, L0_ffn_sh_gate, L0_ffn_sh_up, L0_ffn_sh_down, L0_ffn_eg, L0_ffn_eu, L0_ffn_ed)
    return x

_drawn_inputs = setup_inputs


def setup_inputs(seed=0):
    import zlib

    import numpy as np

    out = dict(_drawn_inputs(seed))
    spreads = {'L0_xattn_bq': (0.0, 0.34),
     'L0_xattn_bk': (0.0, 0.8),
     'L0_xattn_bv': (0.0, 0.1),
     'L0_xattn_bo': (0.0, 0.1)}
    factors = {'L0_ffn_gate_w': 4.356,
     'L0_ffn_sh_gate': 2.757,
     'L0_ffn_sh_up': 2.734,
     'L0_ffn_sh_down': 2.733,
     'L0_ffn_eg': 3.819,
     'L0_ffn_eu': 3.755,
     'L0_ffn_ed': 3.764}
    for name, (base, spread) in spreads.items():
        noise = np.random.default_rng([zlib.crc32(name.encode()), seed]).standard_normal(out[name].shape)
        drawn = base * np.exp(spread * noise) if base else spread * noise
        out[name] = jnp.asarray(drawn.astype(out[name].dtype))
    for name, factor in factors.items():
        out[name] = (out[name] * factor).astype(out[name].dtype)
    return out
```

```python
from contextlib import ExitStack

import concourse.bass as bass
from concourse import mybir

ALU = mybir.AluOpType
ACT = mybir.ActivationFunctionType
AX = mybir.AxisListType
F32 = mybir.dt.float32
F16 = mybir.dt.float16
I32 = mybir.dt.int32

P = 128
RSQRT_LINKS = 12
MAGIC = 1597463007.0


def build(nc, x, ctx_t, wq, bq, wk, bk, wv, bv, wo, bo, gate_t, sh_g, sh_u, sh_d, e_g, e_u, e_d, out):
    B, N, C = x.shape
    CK, BK = ctx_t.shape
    KV = BK // B
    E = e_g.shape[0]
    HD = 16
    D = C // HD
    HF = C // P
    HH = HD // HF
    F = e_g.shape[2] // HF
    FC = F // P
    T = B * N
    NT = T // P
    GT = 4
    GC = GT * P
    NG = NT // GT
    UT = 2
    UC = UT * P
    NU = NT // UT
    UB = NU // B
    JP = 4
    CLIP = 10000.0 * D ** 0.5
    SCALE = D ** -0.5
    EPS = 1e-5
    OW = 2 * D + 2

    x_tiles = x.rearrange("b n c -> (b n) c").rearrange("(t p) c -> p t c", p=P)
    out_tiles = out.rearrange("b n c -> (b n) c").rearrange("(t p) c -> p t c", p=P)

    with ExitStack() as ctx:
        def sb(name, shape, dt):
            return ctx.enter_context(nc.sbuf_tensor(name, shape, dt))

        def sem(name):
            return ctx.enter_context(nc.semaphore(name))

        bank = [ctx.enter_context(nc.psum_tensor(f"bank{i}", [P, 512], F32)) for i in range(8)]

        x_sb = sb("x_sb", [P, NT, C], F32)
        qx = sb("qx", [P, 2, HF, T], F16)
        w_sh = sb("w_sh", [P, 3, 2, 1024], F16)
        arena = sb("arena", [P, E * 3 * 2 * 1024], F16)
        w_rt = arena[:, :].rearrange("p (e m s n) -> p e m s n", e=E, m=3, s=2)
        w_stage = sb("w_stage", [P, 3, 1024], F32)
        logits = sb("logits", [P, NT, E], F32)
        comb = sb("comb", [P, NT, E], F32)
        ident = sb("ident", [P, P], F16)
        gate_hl = sb("gate_hl", [P, 2, HF, E], F16)
        gate_f = sb("gate_f", [P, HF, E], F32)

        used = [0]

        def carve(shape, dt, parts=P):
            n = 1
            for s in shape:
                n *= s
            cols = n * (2 if dt in (F32, I32) else 1)
            a = arena[0:parts, used[0]:used[0] + cols]
            used[0] += (cols + 15) // 16 * 16
            assert used[0] <= E * 3 * 2 * 1024
            if dt != F16:
                a = a.bitcast(dt)
            if len(shape) == 1:
                return a
            names = "abcde"[:len(shape)]
            return a.rearrange(f"p ({' '.join(names)}) -> p {' '.join(names)}",
                               **{k: v for k, v in zip(names, shape)})

        ctx_a = carve([BK], F32)
        ctx_b = carve([BK], F32, CK - P)
        ctx2_a = carve([B, 2, KV], F32)
        ctx2_b = carve([B, 2, KV], F32, CK - P)
        wk_a = carve([C], F32)
        wk_b = carve([C], F32, CK - P)
        wv_a = carve([C], F32)
        wv_b = carve([C], F32, CK - P)
        wq_f = carve([HF, C], F32)
        wo_f = carve([HF, C], F32)
        wq_hl = carve([2, HF, C], F16)
        wo_hl = carve([2, HF, C], F16)
        bq_c = carve([HF], F32)
        bk_c = carve([HF], F32)
        bv_r = carve([C], F32, 1)
        bo_r = carve([C], F32, 1)
        ones_r = carve([P], F32, 1)
        ones_f = carve([P], F32)
        bo_bc = carve([C], F32)
        k_f = carve([HF, BK], F32)
        k_h = carve([HF, BK], F16)
        k_l = carve([HF, BK], F16)
        head_mask = carve([HH], F16)
        k_blk = carve([2, B, HF, HH, KV], F16)
        v_blk_h = carve([B, HD // 2, OW], F16)
        v_blk_l = carve([B, HD // 2, 2 * D], F16)
        neg_ind = carve([HD // 2, 2, KV], F16)
        m_t = carve([T], F16)
        stats = carve([2, GT, 6], F32)
        mean_var = carve([2, GT, 2], F32)
        var_eps = carve([2, GT], F32)
        rstd = carve([2, GT], F32)
        bits = carve([2, GT], I32)
        newton = carve([2, GT], F32)
        q_sum = carve([NG * HF + HF], F32)
        flag = carve([4], F32)
        exp_scale = carve([1], F32)
        carrier = carve([1], F32)
        m_raw = carve([2, GT, HD], F32)
        m_cl = carve([2, GT, HD], F16)
        shared_from = used[0]
        xn = carve([2, GT, C], F32)
        xn_h = carve([2, GT, C], F16)
        xn_l = carve([2, GT, C], F16)
        xn_t = carve([2, 2, HF, GC], F16)
        q_f = carve([2, HF, GC], F32)
        v_f = carve([B, C], F32)
        v_hh = carve([B, C], F16)
        used[0] = shared_from
        p_f = carve([4, 512], F32)
        p_h = carve([4, 512], F16)
        p_l = carve([4, 512], F16)
        r_sum = carve([2, UT, HD], F32)
        o_f = carve([2, UT, C], F32)
        o_h = carve([2, UT, C], F16)
        o_l = carve([2, UT, C], F16)
        o_t = carve([2, UT, 2, HF, P], F16)
        x2 = carve([2, UT, C], F32)
        x2_h = carve([2, UT, C], F16)
        x2_l = carve([2, UT, C], F16)

        rank = sb("rank", [P, E], F32)
        r_a = sb("r_a", [P, NT, E], F32)
        r_b = sb("r_b", [P, NT, E], F32)
        pick1 = sb("pick1", [P, NT, E], F32)
        m1 = sb("m1", [P, NT], F32)
        m2 = sb("m2", [P, NT], F32)
        rk = sb("rk", [P, NT], F32)
        w1 = sb("w1", [P, NT], F32)
        w2 = sb("w2", [P, NT], F32)
        act_g = sb("act_g", [P, 2, GC], F32)
        h_f = sb("h_f", [P, 2, GC], F32)
        h_h = sb("h_h", [P, 2, GC], F16)
        h_l = sb("h_l", [P, 2, GC], F16)

        const_ready = sem("const_ready")
        kv_loaded = sem("kv_loaded")
        x_loaded = [sem("x_loaded0"), sem("x_loaded1")]
        w_loaded = [sem(f"w_loaded{i}") for i in range(3)]
        k_ready = sem("k_ready")
        v_ready = sem("v_ready")
        bo_ready = sem("bo_ready")
        k_copied = sem("k_copied")
        v_copied = sem("v_copied")
        bo_copied = sem("bo_copied")
        proj_split = sem("proj_split")
        kblk_ready = sem("kblk_ready")
        vblk_ready = sem("vblk_ready")
        dve_link = sem("dve_link")
        ln1_link = sem("ln1_link")
        ln2_link = sem("ln2_link")
        xn_ready = sem("xn_ready")
        xnh_ready = sem("xnh_ready")
        xnl_ready = sem("xnl_ready")
        xt_ready = sem("xt_ready")
        xt_copied = sem("xt_copied")
        q_ready = sem("q_ready")
        qf_ready = sem("qf_ready")
        qh_ready = sem("qh_ready")
        ql_ready = sem("ql_ready")
        bo_added = sem("bo_added")
        smax_ready = sem("smax_ready")
        smax_used = sem("smax_used")
        mcl_ready = sem("mcl_ready")
        mt_ready = sem("mt_ready")
        mt_copied = sem("mt_copied")
        flag_ready = sem("flag_ready")
        scale_ready = sem("scale_ready")
        st_scored = sem("st_scored")
        st_clipped = sem("st_clipped")
        st_ready = sem("st_ready")
        exp_ready = sem("exp_ready")
        ph_ready = sem("ph_ready")
        pl_ready = sem("pl_ready")
        pv_ready = sem("pv_ready")
        norm_link = sem("norm_link")
        of_ready = sem("of_ready")
        oh_ready = sem("oh_ready")
        ol_ready = sem("ol_ready")
        ot_ready = sem("ot_ready")
        ot_copied = sem("ot_copied")
        y_ready = sem("y_ready")
        y_added = sem("y_added")
        x2_ready = sem("x2_ready")
        x2h_ready = sem("x2h_ready")
        x2l_ready = sem("x2l_ready")
        x2t_ready = sem("x2t_ready")
        x2t_copied = sem("x2t_copied")
        lg_ready = sem("lg_ready")
        lg_copied = sem("lg_copied")
        route_link = sem("route_link")
        route_exp = sem("route_exp")
        route_in = sem("route_in")
        w_hi = sem("w_hi")
        w_lo = sem("w_lo")
        gu_ready = sem("gu_ready")
        silu_ready = sem("silu_ready")
        hf_ready = sem("hf_ready")
        hh_ready = sem("hh_ready")
        hl_ready = sem("hl_ready")
        down_used = sem("down_used")
        ffn_added = sem("ffn_added")
        out_stored = sem("out_stored")

        block = ctx.enter_context(nc.Block())

        N_KV = 17

        def batches(eng, body):
            body(0)
            with eng.Fori(1, B) as b:
                body(b)

        def run_units(eng, body):
            for s in range(UB):
                body(s, s)
            with eng.Fori(1, B) as b:
                for s in range(UB):
                    body(UB * b + s, s)
            for s in range(3):
                body(NU + s, s)

        def apart(eng, sem_, value, settled, count):
            eng.wait_ge(settled, count)
            eng.wait_ge(sem_, value)

        def known(u, lag):
            return not isinstance(u, int) or 0 <= u - lag < NU

        def rsqrt(dve, link, var, ve, bit, t, y):
            link(dve.tensor_scalar(ve, var, EPS, None, ALU.add))
            link(dve.tensor_scalar(bit, ve.bitcast(I32), 1, None, ALU.logical_shift_right))
            link(dve.tensor_scalar(y.bitcast(I32), bit, -1.0, MAGIC, ALU.mult, ALU.add))
            for _ in range(3):
                link(dve.scalar_tensor_tensor(out=t, in0=y, scalar=-0.5, in1=y, op0=ALU.mult, op1=ALU.mult))
                link(dve.tensor_tensor(t, t, ve, ALU.mult))
                link(dve.scalar_tensor_tensor(out=y, in0=t, scalar=1.5, in1=y, op0=ALU.add, op1=ALU.mult))

        @block.sync
        def _(sp):
            sp.dma_start(ctx_a, ctx_t[0:P, :]).then_inc(kv_loaded, 16)
            sp.dma_start(ctx_b, ctx_t[P:CK, :]).then_inc(kv_loaded, 16)
            sp.dma_start(wk_a, wk[0:P, :]).then_inc(kv_loaded, 16)
            sp.dma_start(wk_b, wk[P:CK, :]).then_inc(kv_loaded, 16)
            sp.dma_start(bk_c, bk).then_inc(kv_loaded, 16)
            sp.dma_start(bq_c, bq).then_inc(kv_loaded, 16)
            for a in range(2):
                sp.dma_start(ctx2_a[:, :, a, :], ctx_t[0:P, :].rearrange("p (b k) -> p b k", b=B)
                             ).then_inc(kv_loaded, 16)
                sp.dma_start(ctx2_b[:, :, a, :], ctx_t[P:CK, :].rearrange("p (b k) -> p b k", b=B)
                             ).then_inc(kv_loaded, 16)
            sp.dma_start(x_sb[:, 0:GT, :], x_tiles[:, 0:GT, :]).then_inc(x_loaded[0], 16)
            sp.dma_start(wq_f, wq.rearrange("(h p) c -> p h c", p=P)).then_inc(kv_loaded, 16)
            sp.dma_start(wv_a, wv[0:P, :]).then_inc(kv_loaded, 16)
            sp.dma_start(wv_b, wv[P:CK, :]).then_inc(kv_loaded, 16)
            sp.dma_start(bv_r, bv.rearrange("(a c) -> a c", a=1)).then_inc(kv_loaded, 16)
            sp.dma_start(bo_r, bo.rearrange("(a c) -> a c", a=1)).then_inc(kv_loaded, 16)
            sp.dma_start(wo_f, wo.rearrange("(h p) c -> p h c", p=P)).then_inc(kv_loaded, 16)
            sp.dma_start(gate_f[:, :, :], gate_t.rearrange("(h p) e -> p h e", p=P)).then_inc(kv_loaded, 16)
            for g in range(1, NG):
                if g >= 2:
                    sp.wait_ge(x_loaded[g % 2], 16 * (g // 2))
                sp.dma_start(x_sb[:, g * GT:(g + 1) * GT, :],
                             x_tiles[:, g * GT:(g + 1) * GT, :]).then_inc(x_loaded[g % 2], 16)
            src = [(sh_g, sh_u, sh_d)] + [(e_g[e], e_u[e], e_d[e]) for e in range(E)]
            for k in range(3 * (E + 1)):
                if k >= 3:
                    sp.wait_ge(w_lo, k - 2)
                sp.dma_start(w_stage[:, k % 3, :], src[k // 3][k % 3]).then_inc(w_loaded[k % 3], 16)
            for g in range(NG):
                sp.wait_ge(ffn_added, E * NG + g + 1)
                sp.dma_start(out_tiles[:, g * GT:(g + 1) * GT, :],
                             x_sb[:, g * GT:(g + 1) * GT, :]).then_inc(out_stored, 16)
            sp.wait_ge(out_stored, 16 * NG)

        @block.gpsimd
        def _(pool):
            pool.memset(ident[:, :], 0.0).then_inc(const_ready, 1)
            pool.memset(head_mask, 1.0).then_inc(const_ready, 1)
            pool.memset(neg_ind, 0.0).then_inc(const_ready, 1)
            pool.memset(ones_r, 1.0).then_inc(const_ready, 1)
            pool.memset(m_t.bitcast(F32), 0.0).then_inc(const_ready, 1)
            pool.memset(ones_f, 1.0).then_inc(const_ready, 1)
            pool.memset(v_blk_h, 0.0).then_inc(const_ready, 1)
            pool.memset(v_blk_l, 0.0).then_inc(const_ready, 1)
            pool.iota(rank[:, :], pattern=[[-1, E]], base=E, channel_multiplier=0,
                      allow_small_or_imprecise_dtypes=True).then_inc(const_ready, 1)
            pool.wait_ge(const_ready, 9)
            pool.affine_select(out=ident[:, :], in_=ident[:, :], compare_op=ALU.not_equal, fill=1.0, base=0,
                               pattern=[[-1, P]], channel_multiplier=1).then_inc(const_ready, 1)
            pool.affine_select(out=head_mask, in_=head_mask, compare_op=ALU.is_ge, fill=0.0, base=0,
                               pattern=[[-D, HH]], channel_multiplier=1).then_inc(const_ready, 1)
            pool.wait_ge(const_ready, 11)
            pool.affine_select(out=head_mask, in_=head_mask, compare_op=ALU.is_ge, fill=0.0, base=D - 1,
                               pattern=[[D, HH]], channel_multiplier=-1).then_inc(const_ready, 1)
            pool.affine_select(out=neg_ind, in_=neg_ind, compare_op=ALU.not_equal, fill=-1.0, base=0,
                               pattern=[[-2, HD // 2], [-1, 2], [0, KV]],
                               channel_multiplier=1).then_inc(const_ready, 1)
            for h2 in range(2):
                pool.wait_ge(const_ready, 13 + h2)
                pool.memset(v_blk_h[h2 * KV:(h2 + 1) * KV, :, :, 2 * D + h2:2 * D + h2 + 1],
                            1.0).then_inc(const_ready, 1)
            pool.wait_ge(bo_copied, 1)

            def phase1(b):
                for s in range(2):
                    n = 2 * b + s
                    pool.wait_ge(xnh_ready, n + 1)
                    if not isinstance(b, int):
                        pool.wait_ge(xt_ready, GT * (n - 1))
                    pool.tensor_tensor(xn_l[:, s], xn[:, s], xn_h[:, s], ALU.subtract).then_inc(xnl_ready, 1)
                    xg = x_sb[:, bass.ts(n, GT), :]
                    pool.tensor_tensor(xg, xg, bo_bc.unsqueeze(1).to_broadcast([P, GT, C]),
                                       ALU.add).then_inc(bo_added, 1)
                    for hf in range(HF):
                        pool.wait_ge(qh_ready, HF * n + hf + 1)
                        pool.tensor_tensor(qx[:, 1, hf, bass.ts(n, GC)], q_f[:, s, hf],
                                           qx[:, 0, hf, bass.ts(n, GC)], ALU.subtract).then_inc(ql_ready, 1)

            batches(pool, phase1)

            def split_lo(k):
                e, m = divmod(k, 3)
                w = w_sh[:, m] if e == 0 else w_rt[:, e - 1, m]
                pool.wait_ge(w_hi, k + 1)
                pool.tensor_tensor(w[:, 1, :], w_stage[:, k % 3, :], w[:, 0, :], ALU.subtract).then_inc(w_lo, 1)

            def phase2(u, s):
                for jp in range(JP):
                    k = JP * u + jp
                    if known(u, 0):
                        pool.wait_ge(ph_ready, k + 1)
                        if not isinstance(u, int) or u > 0:
                            pool.wait_ge(pv_ready, k - 3)
                        pool.tensor_tensor(p_l[:, jp], p_f[:, jp], p_h[:, jp], ALU.subtract).then_inc(pl_ready, 1)
                    if jp == 1 and known(u, 2):
                        pool.wait_ge(x2h_ready, u - 1)
                        if not isinstance(u, int) or u > 3:
                            pool.wait_ge(x2t_ready, u - 3)
                        pool.tensor_tensor(x2_l[:, s % 2], x2[:, s % 2], x2_h[:, s % 2],
                                           ALU.subtract).then_inc(x2l_ready, 1)
                    if jp == 3 and known(u, 1):
                        pool.wait_ge(oh_ready, u)
                        if not isinstance(u, int) or u > 2:
                            pool.wait_ge(ot_ready, u - 2)
                        par = (s + 1) % 2
                        pool.tensor_tensor(o_l[:, par], o_f[:, par], o_h[:, par], ALU.subtract).then_inc(ol_ready, 1)

            run_units(pool, phase2)
            for k in range(3):
                split_lo(k)
            pool.wait_ge(lg_copied, NU)
            for e in range(E + 1):
                if e < E:
                    for m in range(3):
                        split_lo(3 * (e + 1) + m)

        @block.scalar
        def _(act):
            for hf in range(HF):
                act.wait_ge(k_ready, hf + 1)
                act.activation(k_f[:, hf], bank[hf][:, 0:BK], ACT.Identity, bias=bk_c[:, hf:hf + 1],
                               accum_out=q_sum[:, NG * HF + hf:NG * HF + hf + 1]).then_inc(k_copied, 1)
            for b in range(B):
                act.wait_ge(v_ready, b + 1)
                act.copy(v_f[:, b], bank[2 + b][:, 0:C]).then_inc(v_copied, 1)
            act.wait_ge(bo_ready, 1)
            act.copy(bo_bc, bank[6][:, 0:C]).then_inc(bo_copied, 1)

            act.wait_ge(const_ready, 15)

            def phase1(b):
                loop = not isinstance(b, int)
                for s in range(2):
                    n = 2 * b + s
                    act.wait_ge(xn_ready, n + 1)
                    if loop:
                        act.wait_ge(xt_ready, GT * (n - 1))
                    act.copy(xn_h[:, s], xn[:, s]).then_inc(xnh_ready, 1)
                    for i in range(GT):
                        act.wait_ge(xt_ready, GT * n + i + 1)
                        if loop and i == 0:
                            act.wait_ge(q_ready, HF * (n - 1))
                        act.copy(xn_t[:, s, :, :, bass.ts(i, P)],
                                 bank[i % 2][:, 0:256].bitcast(F16).rearrange("p (s h t) -> p s h t", s=2, h=HF)
                                 ).then_inc(xt_copied, 1)
                    for hf in range(HF):
                        act.wait_ge(q_ready, HF * n + hf + 1)
                        if loop:
                            act.wait_ge(ql_ready, HF * (n - 2) + hf + 1)
                        act.activation(q_f[:, s, hf], bank[2 + hf][:, :], ACT.Identity, bias=bq_c[:, hf:hf + 1],
                                       accum_out=q_sum[:, bass.ds(HF * n + hf, 1)]).then_inc(qf_ready, 1)
                        act.wait_ge(qf_ready, HF * n + hf + 1)
                        act.copy(qx[:, 0, hf, bass.ts(n, GC)], q_f[:, s, hf]).then_inc(qh_ready, 1)
                    if loop or s == 1:
                        act.wait_ge(mt_ready, n)
                        act.copy(m_t[0:HD, bass.ts(n - 1, GC)], bank[6][0:HD, 0:256].bitcast(F16)).then_inc(mt_copied, 1)

            batches(act, phase1)
            act.wait_ge(mt_ready, NG)
            act.copy(m_t[0:HD, bass.ts(NG - 1, GC)], bank[6][0:HD, 0:256].bitcast(F16)).then_inc(mt_copied, 1)
            act.wait_ge(scale_ready, 1)

            def phase2(u, s):
                for jp in range(JP):
                    k = JP * u + jp
                    if known(u, 0):
                        act.wait_ge(st_ready, k + 1)
                        if not isinstance(u, int) or u > 0:
                            act.wait_ge(pl_ready, k - 3)
                        act.activation(p_f[:, jp], bank[jp][:, :], ACT.Exp,
                                       scale=exp_scale).then_inc(exp_ready, 1)
                        act.wait_ge(exp_ready, k + 1)
                        if not isinstance(u, int) or u > 0:
                            act.wait_ge(pv_ready, k - 3)
                        act.copy(p_h[:, jp], p_f[:, jp]).then_inc(ph_ready, 1)
                    if jp == 0 and known(u, 2):
                        act.wait_ge(ot_ready, u - 1)
                        if not isinstance(u, int) or u > 3:
                            act.wait_ge(y_ready, u - 3)
                        act.copy(o_t[:, s % 2], bank[6][:, :].bitcast(F16).rearrange(
                            "p (t s h q) -> p t s h q", t=UT, s=2, h=HF)).then_inc(ot_copied, 1)
                    if jp == 1 and known(u, 2):
                        act.wait_ge(x2_ready, u - 1)
                        if not isinstance(u, int) or u > 3:
                            act.wait_ge(x2t_ready, u - 3)
                        act.copy(x2_h[:, s % 2], x2[:, s % 2]).then_inc(x2h_ready, 1)
                    if jp == 2 and known(u, 3):
                        act.wait_ge(x2t_ready, u - 2)
                        for t in range(UT):
                            i = act.copy(qx[:, :, :, bass.ts(UT * (u - 3) + t, P)],
                                         bank[6][:, 256 * t:256 * t + 256].bitcast(F16).rearrange(
                                             "p (s h q) -> p s h q", s=2, h=HF))
                        i.then_inc(x2t_copied, 1)
                    if jp == 3 and known(u, 1):
                        act.wait_ge(of_ready, u)
                        if not isinstance(u, int) or u > 2:
                            act.wait_ge(ot_ready, u - 2)
                        par = (s + 1) % 2
                        act.copy(o_h[:, par], o_f[:, par]).then_inc(oh_ready, 1)

            run_units(act, phase2)

            def split_hi(k):
                e, m = divmod(k, 3)
                w = w_sh[:, m] if e == 0 else w_rt[:, e - 1, m]
                act.wait_ge(w_loaded[k % 3], 16 * (k // 3 + 1))
                act.copy(w[:, 0, :], w_stage[:, k % 3, :]).then_inc(w_hi, 1)

            for k in range(3):
                split_hi(k)
            act.wait_ge(route_in, 1)
            act.activation(w2[:, :], w2[:, :], ACT.Exp).then_inc(route_exp, 1)
            act.wait_ge(lg_copied, NU)

            for e in range(E + 1):
                if e < E:
                    for m in range(3):
                        split_hi(3 * (e + 1) + m)

                def ffn(gp):
                    loop = e > 0 or not isinstance(gp, int)
                    for s in range(2):
                        for hc in range(FC):
                            k = e * NG * FC + 2 * FC * gp + s * FC + hc
                            act.wait_ge(gu_ready, k + 1)
                            if loop or s > 0 or hc > 1:
                                act.wait_ge(hf_ready, k - 1)
                            act.activation(act_g[:, hc % 2], bank[hc % 2][:, :], ACT.Silu).then_inc(silu_ready, 1)
                            act.wait_ge(hf_ready, k + 1)
                            if loop or s > 0 or hc > 1:
                                act.wait_ge(down_used, k - 1)
                            act.copy(h_h[:, hc % 2], h_f[:, hc % 2]).then_inc(hh_ready, 1)

                if e == 0:
                    ffn(0)
                    with act.Fori(1, NG // 2) as gp:
                        ffn(gp)
                else:
                    with act.Fori(0, NG // 2) as gp:
                        ffn(gp)

        @block.vector
        def _(dve):
            links = [0]

            def link(ins):
                links[0] += 1
                ins.then_inc(dve_link, 1)
                dve.wait_ge(dve_link, links[0])

            dve.wait_ge(kv_loaded, 16 * N_KV)
            for w, hl in ((wq_f, wq_hl), (wo_f, wo_hl), (gate_f[:, :, :], gate_hl[:, :, :, :])):
                link(dve.tensor_copy(hl[:, 0], w))
                dve.tensor_tensor(hl[:, 1], w, hl[:, 0], ALU.subtract).then_inc(proj_split, 1)
            dve.wait_ge(k_copied, HF)
            dve.wait_ge(const_ready, 15)
            link(dve.tensor_copy(k_h, k_f))
            link(dve.tensor_tensor(k_l, k_f, k_h, ALU.subtract))
            for sp_, kk in ((0, k_h), (1, k_l)):
                for b in range(B):
                    for hf in range(HF):
                        dve.tensor_tensor(
                            k_blk[:, sp_, b, hf],
                            kk[:, hf, bass.ts(b, KV)].unsqueeze(1).to_broadcast([P, HH, KV]),
                            head_mask.unsqueeze(2).to_broadcast([P, HH, KV]), ALU.mult).then_inc(kblk_ready, 1)
            dve.wait_ge(v_copied, B)
            link(dve.tensor_copy(v_hh, v_f))
            for h2 in range(2):
                r = slice(h2 * KV, (h2 + 1) * KV)
                c = slice(h2 * D, (h2 + 1) * D)
                vf = v_f[r].rearrange("p b (j h d) -> p b j h d", h=2, d=D)[:, :, :, h2, :]
                vh = v_hh[r].rearrange("p b (j h d) -> p b j h d", h=2, d=D)[:, :, :, h2, :]
                dve.tensor_copy(v_blk_h[r, :, :, c], vh).then_inc(vblk_ready, 1)
                dve.tensor_tensor(v_blk_l[r, :, :, c], vf, vh, ALU.subtract).then_inc(vblk_ready, 1)

            LN1_LINKS = 2 * GT + RSQRT_LINKS

            def row_max(n, s):
                for i in range(GT):
                    for hf in range(HF):
                        dve.wait_ge(smax_ready, HF * (GT * n + i) + hf + 1)
                        dve.tensor_reduce(m_raw[:, s, i, bass.ts(hf, HH)],
                                          bank[4 + hf][:, :].rearrange("p (h k) -> p h k", h=HH),
                                          AX.X, ALU.max).then_inc(smax_used, 1)
                dve.wait_ge(smax_used, HF * GT * (n + 1))
                if not (isinstance(n, int) and n < 1):
                    dve.wait_ge(mt_ready, n)
                dve.tensor_scalar(m_cl[:, s], m_raw[:, s], -CLIP, CLIP, ALU.max, ALU.min).then_inc(mcl_ready, 1)

            def phase1(b):
                loop = not isinstance(b, int)
                for s in range(2):
                    n = 2 * b + s
                    seen = [LN1_LINKS * n]

                    def link1(ins, hold=True):
                        seen[0] = seen[0] + 1
                        ins.then_inc(ln1_link, 1)
                        if hold:
                            dve.wait_ge(ln1_link, seen[0])

                    apart(dve, x_loaded[s], 16 * (b + 1), k_copied, HF)
                    for i in range(GT):
                        link1(dve.bn_stats(stats[:, s, i], x_sb[:, bass.ds(GT * n + i, 1), :].squeeze(1)),
                              i == GT - 1)
                    dve.memset(carrier, 0.0)
                    for i in range(GT):
                        link1(dve.bn_aggr(mean_var[:, s, i], stats[:, s, i]), i == GT - 1)
                    rsqrt(dve, link1, mean_var[:, s, :, 1], var_eps[:, s], bits[:, s], newton[:, s], rstd[:, s])
                    if loop:
                        dve.wait_ge(xnl_ready, n - 1)
                    for i in range(GT):
                        ins = dve.tensor_scalar(xn[:, s, i], x_sb[:, bass.ds(GT * n + i, 1), :].squeeze(1),
                                                mean_var[:, s, i, 0:1], rstd[:, s, i:i + 1],
                                                ALU.subtract, ALU.mult)
                    ins.then_inc(xn_ready, 1)
                    if loop or s == 1:
                        row_max(n - 1, 1 - s)

            batches(dve, phase1)
            row_max(NG - 1, 1)
            dve.wait_ge(flag_ready, 1)
            link(dve.tensor_reduce(flag[:, 0:1], bank[7][:, 0:HF * NG + HF], AX.X, ALU.add))
            link(dve.tensor_tensor(flag[:, 1:2], flag[:, 0:1], flag[:, 0:1], ALU.is_equal))
            dve.tensor_scalar(exp_scale, flag[:, 1:2], SCALE, None, ALU.mult).then_inc(scale_ready, 1)

            LN2_LINKS = 2 * UT + RSQRT_LINKS

            def phase2(u, s):
                par2 = s % 2
                seen = [LN2_LINKS * (u - 2)]

                def link2(ins, hold=True):
                    seen[0] = seen[0] + 1
                    ins.then_inc(ln2_link, 1)
                    if hold:
                        dve.wait_ge(ln2_link, seen[0])

                for jp in range(JP):
                    k = JP * u + jp
                    if known(u, 0):
                        dve.wait_ge(st_scored, k + 1)
                        dve.tensor_scalar(bank[jp][:, :], bank[jp][:, :], CLIP, -CLIP, ALU.min,
                                          ALU.max).then_inc(st_clipped, 1)
                    if jp == 1 and known(u, 2):
                        dve.wait_ge(y_ready, u - 1)
                        xu = x_sb[:, bass.ts(u - 2, UT), :]
                        if isinstance(u, int) and u == 2:
                            dve.wait_ge(bo_added, NG)
                        ins = dve.tensor_tensor(xu, xu, bank[7][:, :].rearrange("p (t c) -> p t c", t=UT), ALU.add)
                        ins.then_inc(y_added, 1)
                        apart(dve, y_added, u - 1, k_copied, HF)
                        for t in range(UT):
                            link2(dve.bn_stats(stats[:, par2, t], x_sb[:, bass.ds(UT * (u - 2) + t, 1), :].squeeze(1)),
                                  t == UT - 1)
                        dve.memset(carrier, 0.0)
                        for t in range(UT):
                            link2(dve.bn_aggr(mean_var[:, par2, t], stats[:, par2, t]), t == UT - 1)
                        rsqrt(dve, link2, mean_var[:, par2, 0:UT, 1], var_eps[:, par2, 0:UT],
                              bits[:, par2, 0:UT], newton[:, par2, 0:UT], rstd[:, par2, 0:UT])
                        if not isinstance(u, int) or u > 3:
                            dve.wait_ge(x2l_ready, u - 3)
                        for t in range(UT):
                            ins = dve.tensor_scalar(x2[:, par2, t], x_sb[:, bass.ds(UT * (u - 2) + t, 1), :].squeeze(1),
                                                    mean_var[:, par2, t, 0:1], rstd[:, par2, t:t + 1],
                                                    ALU.subtract, ALU.mult)
                        ins.then_inc(x2_ready, 1)
                    if jp == 2 and known(u, 1):
                        par = (s + 1) % 2
                        dve.wait_ge(pv_ready, JP * u)
                        for t in range(UT):
                            ins = dve.reciprocal(r_sum[:, par, t].rearrange("p (j h) -> p j h", h=2),
                                                 bank[4 + t][:, 0:HD // 2 * OW].rearrange(
                                                     "p (j w) -> p j w", w=OW)[:, :, 2 * D:OW])
                        ins.then_inc(norm_link, 1)
                        dve.wait_ge(norm_link, u)
                        if not isinstance(u, int) or u > 2:
                            dve.wait_ge(ol_ready, u - 2)
                        for t in range(UT):
                            ins = dve.tensor_tensor(
                                o_f[:, par, t].rearrange("p (j h d) -> p j h d", j=HD // 2, h=2),
                                bank[4 + t][:, 0:HD // 2 * OW].rearrange("p (j w) -> p j w", w=OW)
                                [:, :, 0:2 * D].rearrange("p j (h d) -> p j h d", h=2),
                                r_sum[:, par, t].rearrange("p (j h) -> p j h", h=2).unsqueeze(3)
                                .to_broadcast([P, HD // 2, 2, D]), ALU.mult)
                        ins.then_inc(of_ready, 1)
                    if jp == 3 and known(u, 3):
                        dve.wait_ge(lg_ready, u - 2)
                        dve.tensor_copy(logits[:, bass.ts(u - 3, UT), :],
                                        bank[7][:, 0:UT * E].rearrange("p (t e) -> p t e", t=UT)
                                        ).then_inc(lg_copied, 1)

            run_units(dve, phase2)

            rl = [0]

            def link3(ins):
                rl[0] += 1
                ins.then_inc(route_link, 1)
                dve.wait_ge(route_link, rl[0])

            shape = [P, NT, E]
            rank_b = rank[:, :].unsqueeze(1).to_broadcast(shape)
            dve.wait_ge(lg_copied, NU)
            link3(dve.tensor_reduce(m1[:, :], logits[:, :, :], AX.X, ALU.max))
            link3(dve.tensor_tensor(r_a[:, :, :], logits[:, :, :], m1[:, :].unsqueeze(2).to_broadcast(shape),
                                    ALU.is_equal))
            link3(dve.tensor_tensor(r_a[:, :, :], r_a[:, :, :], rank_b, ALU.mult))
            link3(dve.tensor_reduce(rk[:, :], r_a[:, :, :], AX.X, ALU.max))
            link3(dve.tensor_tensor(pick1[:, :, :], rk[:, :].unsqueeze(2).to_broadcast(shape), rank_b, ALU.is_equal))
            link3(dve.scalar_tensor_tensor(out=r_b[:, :, :], in0=pick1[:, :, :], scalar=-3.0e38,
                                           in1=logits[:, :, :], op0=ALU.mult, op1=ALU.add))
            link3(dve.tensor_reduce(m2[:, :], r_b[:, :, :], AX.X, ALU.max))
            link3(dve.tensor_tensor(r_a[:, :, :], r_b[:, :, :], m2[:, :].unsqueeze(2).to_broadcast(shape),
                                    ALU.is_equal))
            link3(dve.tensor_tensor(r_a[:, :, :], r_a[:, :, :], rank_b, ALU.mult))
            link3(dve.tensor_reduce(rk[:, :], r_a[:, :, :], AX.X, ALU.max))
            link3(dve.tensor_tensor(r_b[:, :, :], rk[:, :].unsqueeze(2).to_broadcast(shape), rank_b, ALU.is_equal))
            dve.tensor_tensor(w2[:, :], m2[:, :], m1[:, :], ALU.subtract).then_inc(route_in, 1)
            dve.wait_ge(route_exp, 1)
            link3(dve.tensor_scalar(w1[:, :], w2[:, :], 1.0, None, ALU.add))
            link3(dve.reciprocal(w1[:, :], w1[:, :]))
            link3(dve.tensor_tensor(w2[:, :], w2[:, :], w1[:, :], ALU.mult))
            link3(dve.tensor_tensor(r_a[:, :, :], pick1[:, :, :], w1[:, :].unsqueeze(2).to_broadcast(shape), ALU.mult))
            link3(dve.tensor_tensor(r_b[:, :, :], r_b[:, :, :], w2[:, :].unsqueeze(2).to_broadcast(shape), ALU.mult))
            link3(dve.tensor_tensor(comb[:, :, :], r_a[:, :, :], r_b[:, :, :], ALU.add))

            for e in range(E + 1):
                def add_y(n, par):
                    for i in range(GT):
                        t = GT * n + i
                        xt = x_sb[:, bass.ds(t, 1), :].squeeze(1)
                        y = bank[4 + 2 * par + i // 2][:, bass.ts(i % 2, C)]
                        if e == 0:
                            ins = dve.tensor_tensor(xt, xt, y, ALU.add)
                        else:
                            ins = dve.scalar_tensor_tensor(
                                out=xt, in0=y, scalar=comb[:, bass.ds(t, 1), e - 1:e].squeeze(1),
                                in1=xt, op0=ALU.mult, op1=ALU.add)
                    ins.then_inc(ffn_added, 1)

                def ffn(gp):
                    loop = e > 0 or not isinstance(gp, int)
                    for s in range(2):
                        n = 2 * gp + s
                        for hc in range(FC):
                            k = e * NG * FC + FC * n + hc
                            dve.wait_ge(silu_ready, k + 1)
                            if loop or s > 0 or hc > 1:
                                dve.wait_ge(hl_ready, k - 1)
                            dve.tensor_tensor(h_f[:, hc % 2], bank[2 + hc % 2][:, :], act_g[:, hc % 2],
                                              ALU.mult).then_inc(hf_ready, 1)
                            dve.wait_ge(hh_ready, k + 1)
                            dve.tensor_tensor(h_l[:, hc % 2], h_f[:, hc % 2], h_h[:, hc % 2],
                                              ALU.subtract).then_inc(hl_ready, 1)
                        dve.wait_ge(down_used, FC * (e * NG + n + 1))
                        if e > 0:
                            dve.wait_ge(ffn_added, e * NG + n - (NG - 1))
                        add_y(n, s)

                if e == 0:
                    ffn(0)
                    with dve.Fori(1, NG // 2) as gp:
                        ffn(gp)
                else:
                    with dve.Fori(0, NG // 2) as gp:
                        ffn(gp)

        @block.tensor
        def _(pe):
            def mm(o, a, b, first, last, check=False):
                return pe.matmul(o, a, b, start=first, stop=last, skip_group_check=not check)

            pe.wait_ge(kv_loaded, 16 * N_KV)
            pe.wait_ge(const_ready, 15)
            for hf in range(HF):
                mm(bank[hf][:, 0:BK], wk_a[:, bass.ts(hf, P)], ctx_a, True, False)
                mm(bank[hf][:, 0:BK], wk_b[:, bass.ts(hf, P)], ctx_b, False, True).then_inc(k_ready, 1)
            for b in range(B):
                o = bank[2 + b][:, 0:C]
                mm(o, ctx2_a[:, b].rearrange("p a k -> p (a k)"), wv_a, True, False)
                mm(o, ctx2_b[:, b].rearrange("p a k -> p (a k)"), wv_b, False, False)
                mm(o, ones_r, bv_r, False, True).then_inc(v_ready, 1)
            mm(bank[6][:, 0:C], ones_r, bo_r, True, True).then_inc(bo_ready, 1)
            pe.wait_ge(proj_split, 3)
            pe.wait_ge(kblk_ready, 2 * B * HF)
            pe.wait_ge(v_copied, B)
            pe.wait_ge(bo_copied, 1)

            THREE = ((0, 0), (0, 1), (1, 0))

            def row_scores(b, n, s):
                for i in range(GT):
                    for hf in range(HF):
                        pe.wait_ge(qh_ready, HF * n + hf + 1)
                        if not (isinstance(n, int) and n == 0 and i == 0):
                            pe.wait_ge(smax_used, HF * (GT * n + i) + hf - 1)
                        mm(bank[4 + hf][:, :], qx[:, 0, hf, bass.ts(GT * n + i, P)],
                           k_blk[:, 0, bass.ds(b, 1), hf].rearrange("p a h k -> p (a h k)"),
                           True, True).then_inc(smax_ready, 1)

            def max_t(n, s):
                pe.wait_ge(mcl_ready, n + 1)
                if not (isinstance(n, int) and n == 0):
                    pe.wait_ge(mt_copied, n)
                for i in range(GT):
                    ins = pe.transpose(bank[6][0:HD, 64 * i:64 * i + 64].bitcast(F16), m_cl[:, s, i], ident[:, :])
                ins.then_inc(mt_ready, 1)

            def phase1(b):
                loop = not isinstance(b, int)
                for s in range(2):
                    n = 2 * b + s
                    pe.wait_ge(xnl_ready, n + 1)
                    for i in range(GT):
                        if loop or s > 0 or i > 1:
                            pe.wait_ge(xt_copied, GT * n + i - 1)
                        for sp_ in range(2):
                            src = (xn_h, xn_l)[sp_]
                            for hf in range(HF):
                                c = (sp_ * HF + hf) * 64
                                ins = pe.transpose(bank[i % 2][:, c:c + 64].bitcast(F16),
                                                   src[:, s, i, bass.ts(hf, P)], ident[:, :])
                        ins.then_inc(xt_ready, 1)
                    if loop or s == 1:
                        row_scores(b if s == 1 else b - 1, n - 1, 1 - s)
                    pe.wait_ge(xt_copied, GT * (n + 1))
                    for hf in range(HF):
                        if loop or s > 0:
                            pe.wait_ge(qf_ready, HF * (n - 1) + hf + 1)
                        for i, (a, c) in enumerate(THREE):
                            for cc in range(HF):
                                ins = mm(bank[2 + hf][:, :], wq_hl[:, a, cc, bass.ts(hf, P)], xn_t[:, s, c, cc],
                                         i == 0 and cc == 0, i == 2 and cc == HF - 1)
                        ins.then_inc(q_ready, 1)
                    if loop or s == 1:
                        max_t(n - 1, 1 - s)

            batches(pe, phase1)
            row_scores(B - 1, NG - 1, 1)
            pe.wait_ge(qf_ready, NG * HF)
            mm(bank[7][:, 0:HF * NG + HF], ones_f, q_sum, True, True).then_inc(flag_ready, 1)
            max_t(NG - 1, 1)
            pe.wait_ge(mt_copied, NG)
            pe.wait_ge(ql_ready, NG * HF)
            pe.wait_ge(vblk_ready, 4)
            pe.wait_ge(scale_ready, 1)

            def scores(u, b, jp):
                k = JP * u + jp
                if not isinstance(u, int) or u > 0:
                    pe.wait_ge(exp_ready, k - 3)
                for j2 in range(2):
                    j = 2 * jp + j2
                    hf, r = divmod(j, HH // 2)
                    for i, (a, c) in enumerate(THREE):
                        ins = mm(bank[jp][:, bass.ts(j2, UC)],
                                 k_blk[:, a, bass.ds(b, 1), hf, 2 * r:2 * r + 2, :].rearrange("p a h k -> p (a h k)"),
                                 qx[:, c, hf, bass.ts(u, UC)], j2 == 0 and i == 0, False)
                ins.then_inc(st_scored, 1)

            def subtract_max(u, jp):
                k = JP * u + jp
                pe.wait_ge(st_clipped, k + 1)
                for j2 in range(2):
                    ins = mm(bank[jp][:, bass.ts(j2, UC)],
                             neg_ind[:, 2 * jp + j2].rearrange("p a k -> p (a k)"),
                             m_t[:, bass.ts(u, UC)], False, True)
                ins.then_inc(st_ready, 1)

            def weigh(u, b, jp):
                k = JP * u + jp
                pe.wait_ge(pl_ready, k + 1)
                if jp == 0 and (not isinstance(u, int) or u > 0):
                    pe.wait_ge(of_ready, u)
                for j2 in range(2):
                    j = 2 * jp + j2
                    for t in range(UT):
                        c = bass.ds(j2 * UC + t * P, P)
                        vh = v_blk_h[:, bass.ds(b, 1), j, :].squeeze(1)
                        vl = v_blk_l[:, bass.ds(b, 1), j, :].squeeze(1)
                        mm(bank[4 + t][:, j * OW:j * OW + OW], p_h[:, jp, c], vh, j == 0, False)
                        mm(bank[4 + t][:, j * OW:j * OW + OW], p_l[:, jp, c], vh, False, False)
                        ins = mm(bank[4 + t][:, j * OW:j * OW + 2 * D], p_h[:, jp, c], vl, False, True)
                ins.then_inc(pv_ready, 1)

            def step_of(k_u, jp, back):
                if jp >= back:
                    return k_u, jp - back
                return k_u - 1, jp - back + JP

            def unit(u, s, b, b_prev):
                for jp in range(JP):
                    if known(u, 0):
                        scores(u, b, jp)
                    v, q = step_of(u, jp, 1)
                    if known(v, 0):
                        subtract_max(v, q)
                    v, q = step_of(u, jp, 3)
                    if known(v, 0):
                        weigh(v, b if jp >= 3 else b_prev, q)
                    if jp == 0 and known(u, 2):
                        pe.wait_ge(ol_ready, u - 1)
                        if not isinstance(u, int) or u > 2:
                            if not isinstance(u, int) or u > 3:
                                pe.wait_ge(x2t_copied, u - 3)
                        for t in range(UT):
                            for sp_ in range(2):
                                for hf in range(HF):
                                    c = ((t * 2 + sp_) * HF + hf) * 64
                                    ins = pe.transpose(bank[6][:, c:c + 64].bitcast(F16),
                                                       (o_h, o_l)[sp_][:, s % 2, t, bass.ts(hf, P)], ident[:, :])
                        ins.then_inc(ot_ready, 1)
                    if jp == 1 and known(u, 2):
                        pe.wait_ge(ot_copied, u - 1)
                        if not isinstance(u, int) or u > 3:
                            pe.wait_ge(lg_copied, u - 3)
                        for t in range(UT):
                            for i, (a, c) in enumerate(THREE):
                                for hf in range(HF):
                                    ins = mm(bank[7][:, bass.ts(t, C)], o_t[:, s % 2, t, c, hf], wo_hl[:, a, hf],
                                             t == 0 and i == 0 and hf == 0, i == 2 and hf == HF - 1)
                        ins.then_inc(y_ready, 1)
                    if jp == 2 and known(u, 3):
                        pe.wait_ge(x2l_ready, u - 2)
                        if known(u, 2):
                            pe.wait_ge(ot_copied, u - 1)
                        else:
                            pe.wait_ge(x2t_copied, u - 3)
                        for t in range(UT):
                            for sp_ in range(2):
                                for hf in range(HF):
                                    c = ((t * 2 + sp_) * HF + hf) * 64
                                    ins = pe.transpose(bank[6][:, c:c + 64].bitcast(F16),
                                                       (x2_h, x2_l)[sp_][:, (s + 1) % 2, t, bass.ts(hf, P)],
                                                       ident[:, :])
                        ins.then_inc(x2t_ready, 1)
                    if jp == 3 and known(u, 3):
                        pe.wait_ge(x2t_copied, u - 2)
                        if known(u, 2):
                            pe.wait_ge(y_added, u - 1)
                        else:
                            pe.wait_ge(lg_copied, u - 3)
                        for t in range(UT):
                            for i, (a, c) in enumerate(THREE + ((1, 1),)):
                                for hf in range(HF):
                                    ins = mm(bank[7][:, bass.ts(t, E)], qx[:, c, hf, bass.ts(UT * (u - 3) + t, P)],
                                             gate_hl[:, a, hf, :], t == 0 and i == 0 and hf == 0,
                                             i == 3 and hf == HF - 1)
                        ins.then_inc(lg_ready, 1)

            for s in range(UB):
                unit(s, s, 0, 0)
            with pe.Fori(1, B) as b:
                for s in range(UB):
                    unit(UB * b + s, s, b, b if s > 0 else b - 1)
            for s in range(3):
                unit(NU + s, s, B, B - 1)

            pe.wait_ge(lg_copied, NU)
            for e in range(E + 1):
                w = w_sh[:, :, :, :] if e == 0 else w_rt[:, e - 1]

                def up(n, s, hc):
                    k = e * NG * FC + FC * n + hc
                    if not (isinstance(k, int) and k < 2):
                        pe.wait_ge(hf_ready, k - 1)
                    for m in range(2):
                        for i, (a, c) in enumerate(THREE):
                            for hf in range(HF):
                                ins = mm(bank[2 * m + hc % 2][:, :],
                                         w[:, m, a, hf * F + hc * P:hf * F + hc * P + P],
                                         qx[:, c, hf, bass.ts(n, GC)],
                                         i == 0 and hf == 0, i == 2 and hf == HF - 1)
                    ins.then_inc(gu_ready, 1)

                def down(n, s, hc):
                    k = e * NG * FC + FC * n + hc
                    pe.wait_ge(hl_ready, k + 1)
                    if hc == 0 and not (isinstance(n, int) and e * NG + n < 2):
                        pe.wait_ge(ffn_added, e * NG + n - 1)
                    for t in range(GT):
                        o = bank[4 + 2 * s + t // 2][:, bass.ts(t % 2, C)]
                        for i, (a, c) in enumerate(THREE):
                            ins = mm(o, (h_h, h_l)[c][:, hc % 2, bass.ts(t, P)], w[:, 2, a, bass.ts(hc, C)],
                                     hc == 0 and i == 0 and t % 2 == 0, hc == FC - 1 and i == 2)
                    ins.then_inc(down_used, 1)

                def ffn(gp):
                    for s in range(2):
                        n = 2 * gp + s
                        up(n, s, 0)
                        for hc in range(1, FC):
                            up(n, s, hc)
                            down(n, s, hc - 1)
                        down(n, s, FC - 1)

                pe.wait_ge(w_lo, 3 * (e + 1))
                if e == 0:
                    ffn(0)
                    with pe.Fori(1, NG // 2) as gp:
                        ffn(gp)
                else:
                    with pe.Fori(0, NG // 2) as gp:
                        ffn(gp)


_INS = ['x', 'ctx_768', 'L0_xattn_Wq', 'L0_xattn_bq', 'L0_xattn_Wk', 'L0_xattn_bk', 'L0_xattn_Wv', 'L0_xattn_bv',
        'L0_xattn_Wo', 'L0_xattn_bo', 'L0_ffn_gate_w', 'L0_ffn_sh_gate', 'L0_ffn_sh_up', 'L0_ffn_sh_down',
        'L0_ffn_eg', 'L0_ffn_eu', 'L0_ffn_ed']


def kernel(**inputs):
    import numpy as np
    import concourse.bacc as bacc
    from concourse import mybir as mb
    from concourse.bass_utils import run_bass_kernel_spmd as run

    a = {k: np.asarray(v) for k, v in inputs.items()}

    def rows(w):
        *lead, k, n = w.shape
        return np.swapaxes(w.reshape(*lead, k // 128, 128, n), -3, -2).reshape(*lead, 128, k // 128 * n)

    arrays = {
        'x': a['x'],
        'ctx_t': a['ctx_768'].transpose(2, 0, 1).reshape(a['ctx_768'].shape[2], -1),
        'wq': a['L0_xattn_Wq'], 'bq': a['L0_xattn_bq'].reshape(-1, 128).T, 'wk': a['L0_xattn_Wk'], 'bk': a['L0_xattn_bk'].reshape(-1, 128).T,
        'wv': a['L0_xattn_Wv'], 'bv': a['L0_xattn_bv'], 'wo': a['L0_xattn_Wo'], 'bo': a['L0_xattn_bo'],
        'gate_t': a['L0_ffn_gate_w'].T,
        'sh_g': rows(a['L0_ffn_sh_gate'].T), 'sh_u': rows(a['L0_ffn_sh_up'].T), 'sh_d': rows(a['L0_ffn_sh_down'].T),
        'e_g': rows(a['L0_ffn_eg'].transpose(0, 2, 1)), 'e_u': rows(a['L0_ffn_eu'].transpose(0, 2, 1)),
        'e_d': rows(a['L0_ffn_ed'].transpose(0, 2, 1)),
    }
    arrays = {k: np.ascontiguousarray(v) for k, v in arrays.items()}
    nc = bacc.Bacc("TRN2", target_bir_lowering=False, num_devices=1)
    aps = [nc.dram_tensor(f"in_{k}", v.shape, mb.dt.from_np(v.dtype), kind="ExternalInput").ap()
           for k, v in arrays.items()]
    out = nc.dram_tensor("out_0", a['x'].shape, mb.dt.float32, kind="ExternalOutput").ap()
    build(nc, *aps, out)
    r = run(nc, [{f"in_{k}": v for k, v in arrays.items()}], core_ids=[0])
    return r.results[0]["out_0"]
```

```python
from contextlib import ExitStack

import concourse.bass as bass
from concourse import mybir

ALU = mybir.AluOpType
ACT = mybir.ActivationFunctionType
AX = mybir.AxisListType
F32 = mybir.dt.float32
F16 = mybir.dt.float16
I32 = mybir.dt.int32

P = 128
RSQRT_LINKS = 12
MAGIC = 1597463007.0


def build(nc, x, ctx_t, wq, bq, wk, bk, wv, bv, wo, bo, gate_t, w_all, out):
    B, N, C = x.shape
    CK, BK = ctx_t.shape
    KV = BK // B
    E = w_all.shape[0] // 3 - 1
    HD = 16
    D = C // HD
    HF = C // P
    HH = HD // HF
    F = w_all.shape[2] // HF
    FC = F // P
    T = B * N
    NT = T // P
    GT = 4
    GC = GT * P
    NG = NT // GT
    UT = 2
    UC = UT * P
    NU = NT // UT
    UB = NU // B
    JP = 4
    CLIP = 10000.0 * D ** 0.5
    SCALE = D ** -0.5
    EPS = 1e-5
    TOP = 2
    NS = (TOP * NT + E - 1 + 7) // 8 * 8
    NGB = 6
    OW = 2 * D + 2

    x_tiles = x.rearrange("b n c -> (b n) c").rearrange("(t p) c -> p t c", p=P)
    out_tiles = out.rearrange("b n c -> (b n) c").rearrange("(t p) c -> p t c", p=P)

    with ExitStack() as ctx:
        def sb(name, shape, dt):
            return ctx.enter_context(nc.sbuf_tensor(name, shape, dt))

        def sem(name):
            return ctx.enter_context(nc.semaphore(name))

        bank = [ctx.enter_context(nc.psum_tensor(f"bank{i}", [P, 512], F32)) for i in range(8)]

        x_sb = sb("x_sb", [P, NT, C], F32)
        qx = sb("qx", [P, 2, HF, T], F16)
        w_sh = sb("w_sh", [P, 3, 2, 1024], F16)
        arena = sb("arena", [P, E * 3 * 2 * 1024], F16)
        w_rt = arena[:, :].rearrange("p (e m s n) -> p e m s n", e=E, m=3, s=2)
        w_qs = arena[:, :].rearrange("p (q s n) -> p q s n", q=3 * E, s=2)
        w_stage = sb("w_stage", [P, 4, 1024], F32)
        logits = sb("logits", [P, NT, E], F32)
        tri = sb("tri", [P, P], F16)
        ones_h = sb("ones_h", [P, P], F16)
        tile_step = sb("tile_step", [P, NT], F32)
        slot_no = sb("slot_no", [P, NS], F32)
        slot_row = sb("slot_row", [P, NT, TOP, 4], I32)
        pos_i = sb("pos_i", [P, TOP, NT], I32)
        slot_e = sb("slot_e", [P, NS], I32)
        map_sb = sb("map_sb", [P, 8, 4], I32)
        stage_w = w_stage[:, :, :].rearrange("p a n -> p (a n)")
        xg = stage_w[:, 0:1024].bitcast(F16).rearrange("p (r n) -> p r n", r=4)
        xgt = stage_w[:, 1024:1536].bitcast(F16).rearrange("p (r s h t) -> p r s h t", r=2, s=2, h=HF)
        ht = stage_w[:, 1536:2560].bitcast(F16).rearrange("p (r s f t) -> p r s f t", r=2, s=2, f=FC)
        y_sb = stage_w[:, 2560:3584].rearrange("p (r c) -> p r c", r=4)
        yd = arena[:, 0:4 * 2 * GT * C].bitcast(F32).rearrange("p (r k t c) -> p r k t c", r=2, k=TOP, t=GT)

        rows_d = nc.dram_tensor("rows_d", (T, 2 * C), F16, kind="Internal").ap()
        map_d = nc.dram_tensor("map_d", (NS * P, 4), I32, kind="Internal").ap()
        y_d = nc.dram_tensor("y_d", (TOP * T + NS * P, C), F32, kind="Internal").ap()
        ident = sb("ident", [P, P], F16)
        gate_hl = sb("gate_hl", [P, 2, HF, E], F16)
        gate_f = sb("gate_f", [P, HF, E], F32)

        used = [0]

        def carve(shape, dt, parts=P):
            n = 1
            for s in shape:
                n *= s
            cols = n * (2 if dt in (F32, I32) else 1)
            a = arena[0:parts, used[0]:used[0] + cols]
            used[0] += (cols + 15) // 16 * 16
            assert used[0] <= E * 3 * 2 * 1024
            if dt != F16:
                a = a.bitcast(dt)
            if len(shape) == 1:
                return a
            names = "abcde"[:len(shape)]
            return a.rearrange(f"p ({' '.join(names)}) -> p {' '.join(names)}",
                               **{k: v for k, v in zip(names, shape)})

        ctx_a = carve([BK], F32)
        ctx_b = carve([BK], F32, CK - P)
        ctx2_a = carve([B, 2, KV], F32)
        ctx2_b = carve([B, 2, KV], F32, CK - P)
        wk_a = carve([C], F32)
        wk_b = carve([C], F32, CK - P)
        wv_a = carve([C], F32)
        wv_b = carve([C], F32, CK - P)
        wq_f = carve([HF, C], F32)
        wo_f = carve([HF, C], F32)
        wq_hl = carve([2, HF, C], F16)
        wo_hl = carve([2, HF, C], F16)
        bq_c = carve([HF], F32)
        bk_c = carve([HF], F32)
        bv_r = carve([C], F32, 1)
        bo_r = carve([C], F32, 1)
        ones_r = carve([P], F32, 1)
        ones_f = carve([P], F32)
        bo_bc = carve([C], F32)
        k_f = carve([HF, BK], F32)
        k_h = carve([HF, BK], F16)
        k_l = carve([HF, BK], F16)
        head_mask = carve([HH], F16)
        k_blk = carve([2, B, HF, HH, KV], F16)
        v_blk_h = carve([B, HD // 2, OW], F16)
        v_blk_l = carve([B, HD // 2, 2 * D], F16)
        neg_ind = carve([HD // 2, 2, KV], F16)
        m_t = carve([T], F16)
        stats = carve([2, GT, 6], F32)
        mean_var = carve([2, GT, 2], F32)
        var_eps = carve([2, GT], F32)
        rstd = carve([2, GT], F32)
        bits = carve([2, GT], I32)
        newton = carve([2, GT], F32)
        q_sum = carve([NG * HF + HF], F32)
        flag = carve([4], F32)
        exp_scale = carve([1], F32)
        carrier = carve([1], F32)
        m_raw = carve([2, GT, HD], F32)
        m_cl = carve([2, GT, HD], F16)
        shared_from = used[0]
        xn = carve([2, GT, C], F32)
        xn_h = carve([2, GT, C], F16)
        xn_l = carve([2, GT, C], F16)
        xn_t = carve([2, 2, HF, GC], F16)
        q_f = carve([2, HF, GC], F32)
        v_f = carve([B, C], F32)
        v_hh = carve([B, C], F16)
        used[0] = shared_from
        p_f = carve([4, 512], F32)
        p_h = carve([4, 512], F16)
        p_l = carve([4, 512], F16)
        r_sum = carve([2, UT, HD], F32)
        o_f = carve([2, UT, C], F32)
        o_h = carve([2, UT, C], F16)
        o_l = carve([2, UT, C], F16)
        o_t = carve([2, UT, 2, HF, P], F16)
        x2 = carve([2, UT, C], F32)
        x2_hl = carve([2, UT, 2, C], F16)
        x2_h = x2_hl[:, :, :, 0]
        x2_l = x2_hl[:, :, :, 1]

        rank = sb("rank", [P, E], F32)
        m1 = sb("m1", [P, NT], F32)
        m2 = sb("m2", [P, NT], F32)
        rk = sb("rk", [P, NT], F32)
        w1 = sb("w1", [P, NT], F32)
        w2 = sb("w2", [P, NT], F32)
        n_e = sb("n_e", [P, E], F32)
        before_e = sb("before_e", [P, E], F32)
        tiles_e = sb("tiles_e", [P, E], F32)
        tile_end = sb("tile_end", [P, E], F32)
        base_e = sb("base_e", [P, E], F32)
        pos_f = sb("pos_f", [P, TOP, NT], F32)

        hidden = sb("hidden", [P, 6 * GC], F32)
        act_g = hidden[:, 0:2 * GC].rearrange("p (r n) -> p r n", r=2)
        h_f = hidden[:, 2 * GC:4 * GC].rearrange("p (r n) -> p r n", r=2)
        h_h = hidden[:, 4 * GC:5 * GC].bitcast(F16).rearrange("p (r n) -> p r n", r=2)
        h_l = hidden[:, 5 * GC:6 * GC].bitcast(F16).rearrange("p (r n) -> p r n", r=2)
        route = [hidden[:, a * E * NT:(a + 1) * E * NT] for a in range(10)]
        r_a, r_b, pick1, pick2 = [a.rearrange("p (t e) -> p t e", e=E) for a in route[0:4]]
        run_et, pos_et = [a.rearrange("p (e t) -> p e t", e=E) for a in route[4:6]]
        one_et = route[6]
        pick_et = route[7][:, 0:E * NT // 2].bitcast(F16).rearrange("p (e t) -> p e t", e=E)
        cmp_s = hidden[:, 8 * E * NT:8 * E * NT + NS * (E - 1)].rearrange("p (i e) -> p i e", e=E - 1)

        pad_row = hidden[:, 5 * GC:5 * GC + NS * 4].bitcast(I32).rearrange("p (i w) -> p i w", w=4)

        const_ready = sem("const_ready")
        kv_loaded = sem("kv_loaded")
        x_loaded = [sem("x_loaded0"), sem("x_loaded1")]
        w_loaded = [sem(f"w_loaded{i}") for i in range(4)]
        k_ready = sem("k_ready")
        v_ready = sem("v_ready")
        bo_ready = sem("bo_ready")
        k_copied = sem("k_copied")
        v_copied = sem("v_copied")
        bo_copied = sem("bo_copied")
        proj_split = sem("proj_split")
        kblk_ready = sem("kblk_ready")
        vblk_ready = sem("vblk_ready")
        dve_link = sem("dve_link")
        ln1_link = sem("ln1_link")
        ln2_link = sem("ln2_link")
        xn_ready = sem("xn_ready")
        xnh_ready = sem("xnh_ready")
        xnl_ready = sem("xnl_ready")
        xt_ready = sem("xt_ready")
        xt_copied = sem("xt_copied")
        q_ready = sem("q_ready")
        qf_ready = sem("qf_ready")
        qh_ready = sem("qh_ready")
        ql_ready = sem("ql_ready")
        bo_added = sem("bo_added")
        smax_ready = sem("smax_ready")
        smax_used = sem("smax_used")
        mcl_ready = sem("mcl_ready")
        mt_ready = sem("mt_ready")
        mt_copied = sem("mt_copied")
        flag_ready = sem("flag_ready")
        scale_ready = sem("scale_ready")
        st_scored = sem("st_scored")
        st_clipped = sem("st_clipped")
        st_ready = sem("st_ready")
        exp_ready = sem("exp_ready")
        ph_ready = sem("ph_ready")
        pl_ready = sem("pl_ready")
        pv_ready = sem("pv_ready")
        norm_link = sem("norm_link")
        of_ready = sem("of_ready")
        oh_ready = sem("oh_ready")
        ol_ready = sem("ol_ready")
        ot_ready = sem("ot_ready")
        ot_copied = sem("ot_copied")
        y_ready = sem("y_ready")
        y_added = sem("y_added")
        x2_ready = sem("x2_ready")
        x2h_ready = sem("x2h_ready")
        x2l_ready = sem("x2l_ready")
        x2t_ready = sem("x2t_ready")
        x2t_copied = sem("x2t_copied")
        lg_ready = sem("lg_ready")
        lg_copied = sem("lg_copied")
        route_link = sem("route_link")
        route_exp = sem("route_exp")
        route_in = sem("route_in")
        w_hi = sem("w_hi")
        w_lo = sem("w_lo")
        gu_ready = sem("gu_ready")
        silu_ready = sem("silu_ready")
        hf_ready = sem("hf_ready")
        hh_ready = sem("hh_ready")
        hl_ready = sem("hl_ready")
        down_used = sem("down_used")
        ffn_added = sem("ffn_added")
        out_stored = sem("out_stored")
        pad_stored = sem("pad_stored")
        x2_stored = [sem("x2_stored0"), sem("x2_stored1")]
        pick_ready = sem("pick_ready")
        count_ready = sem("count_ready")
        place_ready = sem("place_ready")
        map_stored = sem("map_stored")
        map_loaded = [sem(f"map_loaded{i}") for i in range(8)]
        x_got = [sem(f"x_got{i}") for i in range(4)]
        y_out = [sem(f"y_out{i}") for i in range(4)]
        sp_xt = sem("sp_xt")
        sp_xt_copied = sem("sp_xt_copied")
        sp_up = sem("sp_up")
        sp_silu = sem("sp_silu")
        sp_h = sem("sp_h")
        sp_hh = sem("sp_hh")
        sp_hl = sem("sp_hl")
        sp_ht = sem("sp_ht")
        sp_ht_copied = sem("sp_ht_copied")
        sp_down = sem("sp_down")
        sp_y = sem("sp_y")
        yd_loaded = [sem("yd_loaded0"), sem("yd_loaded1")]
        yd_link = sem("yd_link")
        fin_ready = sem("fin_ready")

        block = ctx.enter_context(nc.Block())

        LAST_LAG = 5
        N_CONST = 28
        N_KV = 17

        def batches(eng, body):
            body(0)
            with eng.Fori(1, B) as b:
                body(b)

        def run_units(eng, body):
            for u in range(2 * UB):
                body(u, u % UB)
            with eng.Fori(2, B) as b:
                for s in range(UB):
                    body(UB * b + s, s)
            for s in range(LAST_LAG):
                body(NU + s, s % UB)

        def apart(eng, sem_, value, settled, count):
            if not isinstance(value, int):
                value = eng.to_reg(value)
            eng.wait_ge(settled, count)
            eng.wait_ge(sem_, value)

        def run_slots(eng, body):
            for i in range(-1, 8):
                body(i // 8, i % 8)
            with eng.Fori(1, NS // 8 - 1) as it:
                for s in range(8):
                    body(it, s)
            for i in range(NS - 8, NS + 2):
                body(i // 8, i % 8)

        def has(i, ahead):
            return not isinstance(i, int) or 0 <= i + ahead < NS

        def old(u, least):
            return not isinstance(u, int) or u >= least

        def known(u, lag):
            return not isinstance(u, int) or 0 <= u - lag < NU

        def rsqrt(dve, link, var, ve, bit, t, y):
            link(dve.tensor_scalar(ve, var, EPS, None, ALU.add))
            link(dve.tensor_scalar(bit, ve.bitcast(I32), 1, None, ALU.logical_shift_right))
            link(dve.tensor_scalar(y.bitcast(I32), bit, -1.0, MAGIC, ALU.mult, ALU.add))
            for _ in range(3):
                link(dve.scalar_tensor_tensor(out=t, in0=y, scalar=-0.5, in1=y, op0=ALU.mult, op1=ALU.mult))
                link(dve.tensor_tensor(t, t, ve, ALU.mult))
                link(dve.scalar_tensor_tensor(out=y, in0=t, scalar=1.5, in1=y, op0=ALU.add, op1=ALU.mult))

        @block.sync
        def _(sp):
            sp.dma_start(ctx_a, ctx_t[0:P, :]).then_inc(kv_loaded, 16)
            sp.dma_start(ctx_b, ctx_t[P:CK, :]).then_inc(kv_loaded, 16)
            sp.dma_start(wk_a, wk[0:P, :]).then_inc(kv_loaded, 16)
            sp.dma_start(wk_b, wk[P:CK, :]).then_inc(kv_loaded, 16)
            sp.dma_start(bk_c, bk).then_inc(kv_loaded, 16)
            sp.dma_start(bq_c, bq).then_inc(kv_loaded, 16)
            for a in range(2):
                sp.dma_start(ctx2_a[:, :, a, :], ctx_t[0:P, :].rearrange("p (b k) -> p b k", b=B)
                             ).then_inc(kv_loaded, 16)
                sp.dma_start(ctx2_b[:, :, a, :], ctx_t[P:CK, :].rearrange("p (b k) -> p b k", b=B)
                             ).then_inc(kv_loaded, 16)
            sp.dma_start(x_sb[:, 0:GT, :], x_tiles[:, 0:GT, :]).then_inc(x_loaded[0], 16)
            sp.dma_start(wq_f, wq.rearrange("(h p) c -> p h c", p=P)).then_inc(kv_loaded, 16)
            sp.dma_start(wv_a, wv[0:P, :]).then_inc(kv_loaded, 16)
            sp.dma_start(wv_b, wv[P:CK, :]).then_inc(kv_loaded, 16)
            sp.dma_start(bv_r, bv.rearrange("(a c) -> a c", a=1)).then_inc(kv_loaded, 16)
            sp.dma_start(bo_r, bo.rearrange("(a c) -> a c", a=1)).then_inc(kv_loaded, 16)
            sp.dma_start(wo_f, wo.rearrange("(h p) c -> p h c", p=P)).then_inc(kv_loaded, 16)
            sp.dma_start(gate_f[:, :, :], gate_t.rearrange("(h p) e -> p h e", p=P)).then_inc(kv_loaded, 16)
            for g in range(1, NG):
                if g >= 2:
                    sp.wait_ge(x_loaded[g % 2], 16 * (g // 2))
                sp.dma_start(x_sb[:, g * GT:(g + 1) * GT, :],
                             x_tiles[:, g * GT:(g + 1) * GT, :]).then_inc(x_loaded[g % 2], 16)
            sp.wait_ge(const_ready, N_CONST)
            sp.dma_start(map_d.rearrange("(i p) w -> p i w", p=P),
                         pad_row).then_inc(pad_stored, 16)

            def load_w(q):
                if q >= 4:
                    sp.wait_ge(w_lo, q - 3)
                sp.dma_start(w_stage[:, q % 4, :], w_all[q]).then_inc(w_loaded[q % 4], 16)

            for q in range(3):
                load_w(q)

            rows_t = rows_d.rearrange("(t p) c -> p t c", p=P)

            def store_rows(v, s):
                sp.wait_ge(x2l_ready, v + 1)
                sp.dma_start(rows_t[:, bass.ts(v, UT), :],
                             x2_hl[:, s % 2].rearrange("p t a c -> p t (a c)")).then_inc(x2_stored[s % 2], 16)

            for s in range(UB):
                store_rows(s, s)
            with sp.Fori(1, B) as b:
                for s in range(UB):
                    store_rows(UB * b + s, s)
            for q in range(3, 3 * (E + 1)):
                load_w(q)

            sp.wait_ge(map_stored, 16 * TOP * NT)

            def load_map(it, s):
                i = 8 * it + s
                if not isinstance(it, int):
                    sp.wait_ge(y_out[s % 4], 16 * (2 * it + s // 4 - 1))
                sp.dma_start(map_sb[:, s, :], map_d[bass.ts(i, P), :]).then_inc(map_loaded[s], 16)

            for s in range(8):
                load_map(0, s)
            with sp.Fori(1, NS // 8) as it:
                for s in range(8):
                    load_map(it, s)

            for r in range(4):
                sp.wait_ge(y_out[r], 16 * (NS // 4))
            y_t = y_d[0:TOP * T, :].rearrange("(k t p) c -> k p t c", k=TOP, p=P)
            for g in range(NG + 2):
                if g >= 2:
                    sp.wait_ge(fin_ready, g - 1)
                    sp.dma_start(out_tiles[:, (g - 2) * GT:(g - 1) * GT, :],
                                 x_sb[:, (g - 2) * GT:(g - 1) * GT, :]).then_inc(out_stored, 16)
                if g < NG:
                    for k in range(TOP):
                        sp.dma_start(yd[:, g % 2, k], y_t[k, :, g * GT:(g + 1) * GT, :]
                                     ).then_inc(yd_loaded[g % 2], 16)
            sp.wait_ge(out_stored, 16 * NG)

        @block.gpsimd
        def _(pool):
            pool.memset(ident[:, :], 0.0).then_inc(const_ready, 1)
            pool.memset(head_mask, 1.0).then_inc(const_ready, 1)
            pool.memset(neg_ind, 0.0).then_inc(const_ready, 1)
            pool.memset(ones_r, 1.0).then_inc(const_ready, 1)
            pool.memset(m_t.bitcast(F32), 0.0).then_inc(const_ready, 1)
            pool.memset(ones_f, 1.0).then_inc(const_ready, 1)
            pool.memset(v_blk_h, 0.0).then_inc(const_ready, 1)
            pool.memset(v_blk_l, 0.0).then_inc(const_ready, 1)
            pool.iota(rank[:, :], pattern=[[-1, E]], base=E, channel_multiplier=0,
                      allow_small_or_imprecise_dtypes=True).then_inc(const_ready, 1)
            pool.memset(tri[:, :], 1.0).then_inc(const_ready, 1)
            pool.memset(ones_h[:, :], 1.0).then_inc(const_ready, 1)
            pool.memset(one_et, 1.0).then_inc(const_ready, 1)
            pool.memset(pad_row, 0).then_inc(const_ready, 1)
            pool.iota(tile_step[:, :], pattern=[[P, NT]], base=0, channel_multiplier=0,
                      allow_small_or_imprecise_dtypes=True).then_inc(const_ready, 1)
            pool.iota(slot_no[:, :], pattern=[[1, NS]], base=0, channel_multiplier=0,
                      allow_small_or_imprecise_dtypes=True).then_inc(const_ready, 1)
            for k in range(TOP):
                pool.iota(slot_row[:, :, k, 0], pattern=[[P, NT]], base=0, channel_multiplier=1).then_inc(const_ready, 1)
                pool.iota(slot_row[:, :, k, 1], pattern=[[P, NT]], base=k * T,
                          channel_multiplier=1).then_inc(const_ready, 1)
            pool.memset(slot_row[:, :, :, 3], 0).then_inc(const_ready, 1)
            pool.wait_ge(const_ready, 20)
            pool.iota(pad_row[:, :, 1], pattern=[[P, NS]], base=TOP * T, channel_multiplier=1).then_inc(const_ready, 1)
            pool.affine_select(out=tri[:, :], in_=tri[:, :], compare_op=ALU.is_gt, fill=0.0, base=0,
                               pattern=[[1, P]], channel_multiplier=-1).then_inc(const_ready, 1)
            pool.affine_select(out=ident[:, :], in_=ident[:, :], compare_op=ALU.not_equal, fill=1.0, base=0,
                               pattern=[[-1, P]], channel_multiplier=1).then_inc(const_ready, 1)
            pool.affine_select(out=head_mask, in_=head_mask, compare_op=ALU.is_ge, fill=0.0, base=0,
                               pattern=[[-D, HH]], channel_multiplier=1).then_inc(const_ready, 1)
            pool.wait_ge(const_ready, 24)
            pool.affine_select(out=head_mask, in_=head_mask, compare_op=ALU.is_ge, fill=0.0, base=D - 1,
                               pattern=[[D, HH]], channel_multiplier=-1).then_inc(const_ready, 1)
            pool.affine_select(out=neg_ind, in_=neg_ind, compare_op=ALU.not_equal, fill=-1.0, base=0,
                               pattern=[[-2, HD // 2], [-1, 2], [0, KV]],
                               channel_multiplier=1).then_inc(const_ready, 1)
            for h2 in range(2):
                pool.wait_ge(const_ready, N_CONST - 2 + h2)
                pool.memset(v_blk_h[h2 * KV:(h2 + 1) * KV, :, :, 2 * D + h2:2 * D + h2 + 1],
                            1.0).then_inc(const_ready, 1)
            pool.wait_ge(bo_copied, 1)

            def phase1(b):
                for s in range(2):
                    n = 2 * b + s
                    pool.wait_ge(xnh_ready, n + 1)
                    if not isinstance(b, int):
                        pool.wait_ge(xt_ready, GT * (n - 1))
                    pool.tensor_tensor(xn_l[:, s], xn[:, s], xn_h[:, s], ALU.subtract).then_inc(xnl_ready, 1)
                    xg = x_sb[:, bass.ts(n, GT), :]
                    pool.tensor_tensor(xg, xg, bo_bc.unsqueeze(1).to_broadcast([P, GT, C]),
                                       ALU.add).then_inc(bo_added, 1)
                    for hf in range(HF):
                        pool.wait_ge(qh_ready, HF * n + hf + 1)
                        pool.tensor_tensor(qx[:, 1, hf, bass.ts(n, GC)], q_f[:, s, hf],
                                           qx[:, 0, hf, bass.ts(n, GC)], ALU.subtract).then_inc(ql_ready, 1)

            batches(pool, phase1)

            def phase2(u, s):
                for jp in range(JP):
                    k = JP * u + jp
                    if jp == 1 and known(u, 2):
                        par = s % 2
                        pool.wait_ge(oh_ready, u - 1)
                        if old(u, 4):
                            pool.wait_ge(ot_ready, u - 3)
                        pool.tensor_tensor(o_l[:, par], o_f[:, par], o_h[:, par], ALU.subtract).then_inc(ol_ready, 1)
                    if jp == 2 and known(u, 4):
                        par = s % 2
                        pool.wait_ge(x2h_ready, u - 3)
                        if old(u, 6):
                            pool.wait_ge(x2t_ready, u - 5)
                        pool.tensor_tensor(x2_l[:, par], x2[:, par], x2_h[:, par], ALU.subtract).then_inc(x2l_ready, 1)
                    if known(u, 0):
                        pool.wait_ge(ph_ready, k + 1)
                        if old(u, 1):
                            pool.wait_ge(pv_ready, k - 3)
                        pool.tensor_tensor(p_l[:, jp], p_f[:, jp], p_h[:, jp], ALU.subtract).then_inc(pl_ready, 1)

            run_units(pool, phase2)

            pool.wait_ge(pad_stored, 16)
            pool.wait_ge(place_ready, 1)
            for t in range(NT):
                for k in range(TOP):
                    pool.indirect_dma_start(
                        out=map_d, out_offset=bass.IndirectOffsetOnAxis(ap=pos_i[:, k, t:t + 1], axis=0),
                        in_=slot_row[:, t, k, :], in_offset=None).then_inc(map_stored, 16)
            for r in range(2):
                pool.wait_ge(x2_stored[r], 16 * (NU // 2))
            pool.wait_ge(w_lo, 3 * (E + 1))

            def gather(it, s):
                i = 8 * it + s
                apart(pool, map_loaded[s], 16 * (it + 1), place_ready, 1)
                if isinstance(i, int) and i == 4:
                    pool.wait_ge(sp_xt, 1)
                pool.indirect_dma_start(
                    out=xg[:, s % 4], out_offset=None, in_=rows_d,
                    in_offset=bass.IndirectOffsetOnAxis(ap=map_sb[:, s, 0:1], axis=0)).then_inc(x_got[s % 4], 16)

            def scatter(i, s):
                apart(pool, sp_y, i + 1, place_ready, 1)
                pool.indirect_dma_start(
                    out=y_d, out_offset=bass.IndirectOffsetOnAxis(ap=map_sb[:, s, 1:2], axis=0),
                    in_=y_sb[:, s % 4], in_offset=None).then_inc(y_out[s % 4], 16)

            for s in range(8):
                gather(0, s)
                if s >= 4:
                    scatter(s - 4, s - 4)
            with pool.Fori(1, NS // 8) as it:
                for s in range(8):
                    gather(it, s)
                    scatter(8 * it + s - 4, (s + 4) % 8)
            for i in range(NS - 4, NS):
                scatter(i, i % 8)

        @block.scalar
        def _(act):
            for hf in range(HF):
                act.wait_ge(k_ready, hf + 1)
                act.activation(k_f[:, hf], bank[hf][:, 0:BK], ACT.Identity, bias=bk_c[:, hf:hf + 1],
                               accum_out=q_sum[:, NG * HF + hf:NG * HF + hf + 1]).then_inc(k_copied, 1)
            for b in range(B):
                act.wait_ge(v_ready, b + 1)
                act.copy(v_f[:, b], bank[2 + b][:, 0:C]).then_inc(v_copied, 1)
            act.wait_ge(bo_ready, 1)
            act.copy(bo_bc, bank[6][:, 0:C]).then_inc(bo_copied, 1)

            act.wait_ge(const_ready, N_CONST)

            def phase1(b):
                loop = not isinstance(b, int)
                for s in range(2):
                    n = 2 * b + s
                    act.wait_ge(xn_ready, n + 1)
                    if loop:
                        act.wait_ge(xt_ready, GT * (n - 1))
                    act.copy(xn_h[:, s], xn[:, s]).then_inc(xnh_ready, 1)
                    for i in range(GT):
                        act.wait_ge(xt_ready, GT * n + i + 1)
                        if loop and i == 0:
                            act.wait_ge(q_ready, HF * (n - 1))
                        act.copy(xn_t[:, s, :, :, bass.ts(i, P)],
                                 bank[i % 2][:, 0:256].bitcast(F16).rearrange("p (s h t) -> p s h t", s=2, h=HF)
                                 ).then_inc(xt_copied, 1)
                    for hf in range(HF):
                        act.wait_ge(q_ready, HF * n + hf + 1)
                        if loop:
                            act.wait_ge(ql_ready, HF * (n - 2) + hf + 1)
                        act.activation(q_f[:, s, hf], bank[2 + hf][:, :], ACT.Identity, bias=bq_c[:, hf:hf + 1],
                                       accum_out=q_sum[:, bass.ds(HF * n + hf, 1)]).then_inc(qf_ready, 1)
                        act.wait_ge(qf_ready, HF * n + hf + 1)
                        act.copy(qx[:, 0, hf, bass.ts(n, GC)], q_f[:, s, hf]).then_inc(qh_ready, 1)
                    if loop or s == 1:
                        act.wait_ge(mt_ready, n)
                        act.copy(m_t[0:HD, bass.ts(n - 1, GC)], bank[6][0:HD, 0:256].bitcast(F16)).then_inc(mt_copied, 1)

            batches(act, phase1)
            act.wait_ge(mt_ready, NG)
            act.copy(m_t[0:HD, bass.ts(NG - 1, GC)], bank[6][0:HD, 0:256].bitcast(F16)).then_inc(mt_copied, 1)
            act.wait_ge(scale_ready, 1)

            def phase2(u, s):
                for jp in range(JP):
                    k = JP * u + jp
                    if jp == 0 and known(u, 2):
                        act.wait_ge(of_ready, u - 1)
                        if old(u, 4):
                            act.wait_ge(ot_ready, u - 3)
                        act.copy(o_h[:, s % 2], o_f[:, s % 2]).then_inc(oh_ready, 1)
                    if jp == 0 and known(u, 4):
                        act.wait_ge(x2_ready, u - 3)
                        if old(u, 6):
                            act.wait_ge(x2t_ready, u - 5)
                            act.wait_ge(x2_stored[s % 2], 8 * (u - s % 2 - 4))
                        act.copy(x2_h[:, s % 2], x2[:, s % 2]).then_inc(x2h_ready, 1)
                    if jp == 1 and known(u, 5):
                        act.wait_ge(x2t_ready, u - 4)
                        for t in range(UT):
                            i = act.copy(qx[:, :, :, bass.ts(UT * (u - 5) + t, P)],
                                         bank[6][:, 256 * t:256 * t + 256].bitcast(F16).rearrange(
                                             "p (s h q) -> p s h q", s=2, h=HF))
                        i.then_inc(x2t_copied, 1)
                    if jp == 3 and known(u, 2):
                        act.wait_ge(ot_ready, u - 1)
                        if old(u, 4):
                            act.wait_ge(y_ready, u - 3)
                        act.copy(o_t[:, s % 2], bank[6][:, :].bitcast(F16).rearrange(
                            "p (t s h q) -> p t s h q", t=UT, s=2, h=HF)).then_inc(ot_copied, 1)
                    if known(u, 0):
                        act.wait_ge(st_ready, k + 1)
                        if old(u, 1):
                            act.wait_ge(pl_ready, k - 3)
                        act.activation(p_f[:, jp], bank[jp][:, :], ACT.Exp,
                                       scale=exp_scale).then_inc(exp_ready, 1)
                        act.wait_ge(exp_ready, k + 1)
                        if old(u, 1):
                            act.wait_ge(pv_ready, k - 3)
                        act.copy(p_h[:, jp], p_f[:, jp]).then_inc(ph_ready, 1)

            run_units(act, phase2)

            def split_hi(w, q, turn):
                act.wait_ge(w_loaded[q], 16 * turn)
                act.copy(w, w_stage[:, q, :]).then_inc(w_hi, 1)

            for q in range(3):
                split_hi(w_sh[:, q, 0, :], q, 1)
            act.wait_ge(route_in, 1)
            act.activation(w2[:, :], w2[:, :], ACT.Exp).then_inc(route_exp, 1)
            act.wait_ge(lg_copied, NU)
            for r in range(2):
                act.wait_ge(x2_stored[r], 16 * (NU // 2))

            def shared(gp, split):
                loop = not isinstance(gp, int) or gp > 0
                for s in range(2):
                    for hc in range(FC):
                        k = 2 * FC * gp + s * FC + hc
                        act.wait_ge(gu_ready, k + 1)
                        if loop or s > 0 or hc > 1:
                            act.wait_ge(hf_ready, k - 1)
                        act.activation(act_g[:, hc % 2], bank[hc % 2][:, :], ACT.Silu).then_inc(silu_ready, 1)
                        if split:
                            q = s * FC + hc
                            split_hi(w_qs[:, bass.ds(k, 1), 0, :].squeeze(1), (q + 3) % 4,
                                     2 * gp + (q + 3) // 4 + 1)
                        act.wait_ge(hf_ready, k + 1)
                        if loop or s > 0 or hc > 1:
                            act.wait_ge(down_used, k - 1)
                        act.copy(h_h[:, hc % 2], h_f[:, hc % 2]).then_inc(hh_ready, 1)

            shared(0, True)
            with act.Fori(1, NGB // 2) as gp:
                shared(gp, True)

            act.wait_ge(w_lo, 3 * (E + 1))
            act.wait_ge(down_used, FC * NGB)

            def slot(it, s):
                i = 8 * it + s
                if has(i, 1):
                    r = (s + 1) % 2
                    act.wait_ge(sp_xt, i + 2)
                    if old(i, 1):
                        act.wait_ge(sp_up, i)
                    act.copy(xgt[:, r], bank[4][:, 0:256].bitcast(F16).rearrange(
                        "p (s h t) -> p s h t", s=2, h=HF)).then_inc(sp_xt_copied, 1)
                if has(i, 0):
                    act.wait_ge(sp_up, i + 1)
                    if old(i, 2):
                        act.wait_ge(sp_h, i - 1)
                    act.activation(act_g[:, s % 2], bank[s % 2][:, :], ACT.Silu).then_inc(sp_silu, 1)
                if has(i, -1):
                    r = (s + 1) % 2
                    act.wait_ge(sp_ht, i)
                    if old(i, 3):
                        act.wait_ge(sp_down, i - 2)
                    act.copy(ht[:, r], bank[5][:, :].bitcast(F16).rearrange(
                        "p (s f t) -> p s f t", s=2, f=FC)).then_inc(sp_ht_copied, 1)
                if has(i, 0):
                    act.wait_ge(sp_h, i + 1)
                    if old(i, 2):
                        act.wait_ge(sp_ht, i - 1)
                    act.copy(h_h[:, s % 2], h_f[:, s % 2]).then_inc(sp_hh, 1)

            run_slots(act, slot)
            shared(NGB // 2, False)

        @block.vector
        def _(dve):
            links = [0]

            def link(ins):
                links[0] += 1
                ins.then_inc(dve_link, 1)
                dve.wait_ge(dve_link, links[0])

            dve.wait_ge(kv_loaded, 16 * N_KV)
            for w, hl in ((wq_f, wq_hl), (wo_f, wo_hl), (gate_f[:, :, :], gate_hl[:, :, :, :])):
                link(dve.tensor_copy(hl[:, 0], w))
                dve.tensor_tensor(hl[:, 1], w, hl[:, 0], ALU.subtract).then_inc(proj_split, 1)
            dve.wait_ge(k_copied, HF)
            dve.wait_ge(const_ready, N_CONST)
            link(dve.tensor_copy(k_h, k_f))
            link(dve.tensor_tensor(k_l, k_f, k_h, ALU.subtract))
            for sp_, kk in ((0, k_h), (1, k_l)):
                for b in range(B):
                    for hf in range(HF):
                        dve.tensor_tensor(
                            k_blk[:, sp_, b, hf],
                            kk[:, hf, bass.ts(b, KV)].unsqueeze(1).to_broadcast([P, HH, KV]),
                            head_mask.unsqueeze(2).to_broadcast([P, HH, KV]), ALU.mult).then_inc(kblk_ready, 1)
            dve.wait_ge(v_copied, B)
            link(dve.tensor_copy(v_hh, v_f))
            for h2 in range(2):
                r = slice(h2 * KV, (h2 + 1) * KV)
                c = slice(h2 * D, (h2 + 1) * D)
                vf = v_f[r].rearrange("p b (j h d) -> p b j h d", h=2, d=D)[:, :, :, h2, :]
                vh = v_hh[r].rearrange("p b (j h d) -> p b j h d", h=2, d=D)[:, :, :, h2, :]
                dve.tensor_copy(v_blk_h[r, :, :, c], vh).then_inc(vblk_ready, 1)
                dve.tensor_tensor(v_blk_l[r, :, :, c], vf, vh, ALU.subtract).then_inc(vblk_ready, 1)

            LN1_LINKS = 2 * GT + RSQRT_LINKS

            def row_max(n, s):
                for i in range(GT):
                    for hf in range(HF):
                        dve.wait_ge(smax_ready, HF * (GT * n + i) + hf + 1)
                        dve.tensor_reduce(m_raw[:, s, i, bass.ts(hf, HH)],
                                          bank[4 + hf][:, :].rearrange("p (h k) -> p h k", h=HH),
                                          AX.X, ALU.max).then_inc(smax_used, 1)
                dve.wait_ge(smax_used, HF * GT * (n + 1))
                if not (isinstance(n, int) and n < 1):
                    dve.wait_ge(mt_ready, n)
                dve.tensor_scalar(m_cl[:, s], m_raw[:, s], -CLIP, CLIP, ALU.max, ALU.min).then_inc(mcl_ready, 1)

            def phase1(b):
                loop = not isinstance(b, int)
                for s in range(2):
                    n = 2 * b + s
                    seen = [LN1_LINKS * n]

                    def link1(ins, hold=True):
                        seen[0] = seen[0] + 1
                        ins.then_inc(ln1_link, 1)
                        if hold:
                            dve.wait_ge(ln1_link, seen[0])

                    apart(dve, x_loaded[s], 16 * (b + 1), k_copied, HF)
                    for i in range(GT):
                        link1(dve.bn_stats(stats[:, s, i], x_sb[:, bass.ds(GT * n + i, 1), :].squeeze(1)),
                              i == GT - 1)
                    dve.memset(carrier, 0.0)
                    for i in range(GT):
                        link1(dve.bn_aggr(mean_var[:, s, i], stats[:, s, i]), i == GT - 1)
                    rsqrt(dve, link1, mean_var[:, s, :, 1], var_eps[:, s], bits[:, s], newton[:, s], rstd[:, s])
                    if loop:
                        dve.wait_ge(xnl_ready, n - 1)
                    for i in range(GT):
                        ins = dve.tensor_scalar(xn[:, s, i], x_sb[:, bass.ds(GT * n + i, 1), :].squeeze(1),
                                                mean_var[:, s, i, 0:1], rstd[:, s, i:i + 1],
                                                ALU.subtract, ALU.mult)
                    ins.then_inc(xn_ready, 1)
                    if loop or s == 1:
                        row_max(n - 1, 1 - s)

            batches(dve, phase1)
            row_max(NG - 1, 1)
            dve.wait_ge(flag_ready, 1)
            link(dve.tensor_reduce(flag[:, 0:1], bank[7][:, 0:HF * NG + HF], AX.X, ALU.add))
            link(dve.tensor_tensor(flag[:, 1:2], flag[:, 0:1], flag[:, 0:1], ALU.is_equal))
            dve.tensor_scalar(exp_scale, flag[:, 1:2], SCALE, None, ALU.mult).then_inc(scale_ready, 1)

            LN2_LINKS = 2 * UT + RSQRT_LINKS

            def phase2(u, s):
                seen = [LN2_LINKS * (u - 3)]

                def link2(ins, hold=True):
                    seen[0] = seen[0] + 1
                    ins.then_inc(ln2_link, 1)
                    if hold:
                        dve.wait_ge(ln2_link, seen[0])

                for jp in range(JP):
                    k = JP * u + jp
                    par = (s + 1) % 2
                    if jp == 1 and known(u, 3):
                        dve.wait_ge(y_ready, u - 2)
                        xu = x_sb[:, bass.ts(u - 3, UT), :]
                        if isinstance(u, int) and u == 3:
                            dve.wait_ge(bo_added, NG)
                        ins = dve.tensor_tensor(xu, xu, bank[7][:, :].rearrange("p (t c) -> p t c", t=UT), ALU.add)
                        ins.then_inc(y_added, 1)
                        apart(dve, y_added, u - 2, k_copied, HF)
                        for t in range(UT):
                            link2(dve.bn_stats(stats[:, par, t], x_sb[:, bass.ds(UT * (u - 3) + t, 1), :].squeeze(1)),
                                  t == UT - 1)
                    if jp == 2 and known(u, 3):
                        dve.memset(carrier, 0.0)
                        for t in range(UT):
                            link2(dve.bn_aggr(mean_var[:, par, t], stats[:, par, t]), t == UT - 1)
                        rsqrt(dve, link2, mean_var[:, par, 0:UT, 1], var_eps[:, par, 0:UT],
                              bits[:, par, 0:UT], newton[:, par, 0:UT], rstd[:, par, 0:UT])
                    if jp == 3 and known(u, 3):
                        if old(u, 5):
                            dve.wait_ge(x2l_ready, u - 4)
                        for t in range(UT):
                            ins = dve.tensor_scalar(x2[:, par, t], x_sb[:, bass.ds(UT * (u - 3) + t, 1), :].squeeze(1),
                                                    mean_var[:, par, t, 0:1], rstd[:, par, t:t + 1],
                                                    ALU.subtract, ALU.mult)
                        ins.then_inc(x2_ready, 1)
                    if jp == 3 and known(u, 1):
                        dve.wait_ge(pv_ready, JP * u)
                        for t in range(UT):
                            ins = dve.reciprocal(r_sum[:, par, t].rearrange("p (j h) -> p j h", h=2),
                                                 bank[4 + t][:, 0:HD // 2 * OW].rearrange(
                                                     "p (j w) -> p j w", w=OW)[:, :, 2 * D:OW])
                        ins.then_inc(norm_link, 1)
                        dve.wait_ge(norm_link, u)
                        if old(u, 3):
                            dve.wait_ge(ol_ready, u - 2)
                        for t in range(UT):
                            ins = dve.tensor_tensor(
                                o_f[:, par, t].rearrange("p (j h d) -> p j h d", j=HD // 2, h=2),
                                bank[4 + t][:, 0:HD // 2 * OW].rearrange("p (j w) -> p j w", w=OW)
                                [:, :, 0:2 * D].rearrange("p j (h d) -> p j h d", h=2),
                                r_sum[:, par, t].rearrange("p (j h) -> p j h", h=2).unsqueeze(3)
                                .to_broadcast([P, HD // 2, 2, D]), ALU.mult)
                        ins.then_inc(of_ready, 1)
                    if known(u, 0):
                        dve.wait_ge(st_scored, k + 1)
                        dve.tensor_scalar(bank[jp][:, :], bank[jp][:, :], CLIP, -CLIP, ALU.min,
                                          ALU.max).then_inc(st_clipped, 1)
                    if jp == 3 and known(u, 5):
                        dve.wait_ge(lg_ready, u - 4)
                        dve.tensor_copy(logits[:, bass.ts(u - 5, UT), :],
                                        bank[7][:, 0:UT * E].rearrange("p (t e) -> p t e", t=UT)
                                        ).then_inc(lg_copied, 1)

            run_units(dve, phase2)

            rl = [0]

            def link3(ins):
                rl[0] += 1
                ins.then_inc(route_link, 1)
                dve.wait_ge(route_link, rl[0])

            shape = [P, NT, E]
            rank_b = rank[:, :].unsqueeze(1).to_broadcast(shape)
            dve.wait_ge(lg_copied, NU)
            dve.wait_ge(pad_stored, 16)
            link3(dve.tensor_reduce(m1[:, :], logits[:, :, :], AX.X, ALU.max))
            link3(dve.tensor_tensor(r_a, logits[:, :, :], m1[:, :].unsqueeze(2).to_broadcast(shape),
                                    ALU.is_equal))
            link3(dve.tensor_tensor(r_a, r_a, rank_b, ALU.mult))
            link3(dve.tensor_reduce(rk[:, :], r_a, AX.X, ALU.max))
            link3(dve.scalar_tensor_tensor(out=pick1, in0=rk[:, :].unsqueeze(2).to_broadcast(shape),
                                           scalar=1.0, in1=rank_b, op0=ALU.max, op1=ALU.is_equal))
            link3(dve.scalar_tensor_tensor(out=r_b, in0=pick1, scalar=-3.0e38,
                                           in1=logits[:, :, :], op0=ALU.mult, op1=ALU.add))
            link3(dve.tensor_reduce(m2[:, :], r_b, AX.X, ALU.max))
            link3(dve.tensor_tensor(r_a, r_b, m2[:, :].unsqueeze(2).to_broadcast(shape),
                                    ALU.is_equal))
            link3(dve.tensor_tensor(r_a, r_a, rank_b, ALU.mult))
            link3(dve.tensor_reduce(rk[:, :], r_a, AX.X, ALU.max))
            link3(dve.scalar_tensor_tensor(out=pick2, in0=rk[:, :].unsqueeze(2).to_broadcast(shape),
                                           scalar=1.0, in1=rank_b, op0=ALU.max, op1=ALU.is_equal))
            dve.tensor_tensor(pick_et.rearrange("p e t -> p t e"), pick1, pick2,
                              ALU.add).then_inc(pick_ready, 1)
            dve.tensor_tensor(w2[:, :], m2[:, :], m1[:, :], ALU.subtract).then_inc(route_in, 1)
            dve.wait_ge(route_exp, 1)
            link3(dve.tensor_scalar(w1[:, :], w2[:, :], 1.0, None, ALU.add))
            link3(dve.reciprocal(w1[:, :], w1[:, :]))
            link3(dve.tensor_copy(slot_row[:, :, 0, 2].bitcast(F32), w1[:, :]))
            link3(dve.tensor_tensor(slot_row[:, :, 1, 2].bitcast(F32), w2[:, :], w1[:, :], ALU.mult))

            et = [P, E, NT]
            flat = "p e t -> p (e t)"
            dve.wait_ge(count_ready, 1)
            in_tile = bank[7][:, E * NT:2 * E * NT].rearrange("p (e t) -> p e t", e=E)
            before = bank[7][:, 0:E * NT].rearrange("p (e t) -> p e t", e=E)
            link3(dve.tensor_tensor_scan(run_et.rearrange(flat), one_et,
                                         bank[7][:, E * NT:2 * E * NT], 0.0, ALU.mult, ALU.add))
            ends = run_et[:, :, NT - 1]
            link3(dve.memset(before_e[:, 0:1], 0.0))
            link3(dve.tensor_copy(before_e[:, 1:E], ends[:, 0:E - 1]))
            link3(dve.tensor_tensor(n_e[:, :], ends, before_e[:, :], ALU.subtract))
            link3(dve.tensor_tensor(pos_et, n_e[:, :].unsqueeze(2).to_broadcast(et),
                                    tile_step[:, :].unsqueeze(1).to_broadcast(et), ALU.is_gt))
            link3(dve.tensor_reduce(tiles_e[:, :], pos_et, AX.X, ALU.add))
            link3(dve.tensor_tensor_scan(tile_end[:, :], one_et[:, 0:E], tiles_e[:, :], 0.0, ALU.mult, ALU.add))
            link3(dve.tensor_tensor(base_e[:, :], tile_end[:, :], tiles_e[:, :], ALU.subtract))
            link3(dve.scalar_tensor_tensor(out=base_e[:, :], in0=base_e[:, :], scalar=float(P),
                                           in1=before_e[:, :], op0=ALU.mult, op1=ALU.subtract))
            link3(dve.tensor_tensor(pos_et, run_et, in_tile, ALU.subtract))
            link3(dve.tensor_tensor(pos_et, pos_et, before, ALU.add))
            link3(dve.tensor_tensor(pos_et, pos_et, base_e[:, :].unsqueeze(2).to_broadcast(et),
                                    ALU.add))
            for k, pick in enumerate((pick1, pick2)):
                link3(dve.tensor_tensor(r_a, pick[:, :, :], pos_et.rearrange("p e t -> p t e"),
                                        ALU.mult))
                link3(dve.tensor_reduce(pos_f[:, k], r_a, AX.X, ALU.add))
            link3(dve.tensor_copy(pos_i[:, :, :], pos_f[:, :, :]))
            se = [P, NS, E - 1]
            link3(dve.tensor_tensor(cmp_s, tile_end[:, 0:E - 1].unsqueeze(1).to_broadcast(se),
                                    slot_no[:, :].unsqueeze(2).to_broadcast(se), ALU.is_le))
            link3(dve.tensor_reduce(pos_et.rearrange(flat)[:, 0:NS], cmp_s, AX.X, ALU.add))
            dve.tensor_copy(slot_e[:, :], pos_et.rearrange(flat)[:, 0:NS]).then_inc(place_ready, 1)

            def split_lo(w, w_high, q, count):
                dve.wait_ge(w_hi, count)
                dve.tensor_tensor(w, w_stage[:, q, :], w_high, ALU.subtract).then_inc(w_lo, 1)

            for q in range(3):
                split_lo(w_sh[:, q, 1, :], w_sh[:, q, 0, :], q, q + 1)

            def shared(gp, split, between=None):
                loop = not isinstance(gp, int) or gp > 0
                for s in range(2):
                    n = 2 * gp + s
                    for hc in range(FC):
                        k = FC * n + hc
                        dve.wait_ge(silu_ready, k + 1)
                        if loop or s > 0 or hc > 1:
                            dve.wait_ge(hl_ready, k - 1)
                        dve.tensor_tensor(h_f[:, hc % 2], bank[2 + hc % 2][:, :], act_g[:, hc % 2],
                                          ALU.mult).then_inc(hf_ready, 1)
                        if split:
                            w = w_qs[:, bass.ds(k, 1), :, :].squeeze(1)
                            split_lo(w[:, 1], w[:, 0], (s * FC + hc + 3) % 4, k + 4)
                        dve.wait_ge(hh_ready, k + 1)
                        if loop or s > 0 or hc > 1:
                            dve.wait_ge(down_used, k - 1)
                        dve.tensor_tensor(h_l[:, hc % 2], h_f[:, hc % 2], h_h[:, hc % 2],
                                          ALU.subtract).then_inc(hl_ready, 1)
                        if between is not None:
                            between()
                    dve.wait_ge(down_used, FC * (n + 1))
                    for i in range(GT // 2):
                        xt = x_sb[:, bass.ds(GT * n + 2 * i, 2), :]
                        ins = dve.tensor_tensor(xt, xt, bank[4 + 2 * s + i][:, :].rearrange(
                            "p (t c) -> p t c", t=2), ALU.add)
                    ins.then_inc(ffn_added, 1)

            shared(0, True)
            with dve.Fori(1, NGB // 2) as gp:
                shared(gp, True)

            def slot(it, s):
                i = 8 * it + s
                if has(i, 0):
                    dve.wait_ge(sp_silu, i + 1)
                    if old(i, 2):
                        dve.wait_ge(sp_hh, i - 1)
                    dve.tensor_tensor(h_f[:, s % 2], bank[2 + s % 2][:, :], act_g[:, s % 2],
                                      ALU.mult).then_inc(sp_h, 1)
                if has(i, -2):
                    r = (s + 2) % 4
                    dve.wait_ge(sp_down, i - 1)
                    if old(i, 6):
                        dve.wait_ge(y_out[r], 16 * (2 * it + (s - 2) // 4))
                    m = (s - 2) % 8
                    dve.wait_ge(map_loaded[m], 16 * (it + (s - 2) // 8 + 1))
                    dve.tensor_scalar(y_sb[:, r], bank[6 + s % 2][:, 0:C], map_sb[:, m, 2:3].bitcast(F32),
                                      None, ALU.mult).then_inc(sp_y, 1)
                if has(i, 0):
                    dve.wait_ge(sp_hh, i + 1)
                    if old(i, 2):
                        dve.wait_ge(sp_ht, i - 1)
                    dve.tensor_tensor(h_l[:, s % 2], h_f[:, s % 2], h_h[:, s % 2],
                                      ALU.subtract).then_inc(sp_hl, 1)

            run_slots(dve, slot)

            done = [0]

            def finish():
                g = done[0]
                if g >= NG:
                    return
                done[0] = g + 1
                xv = x_sb[:, g * GT:(g + 1) * GT, :]
                if g >= NGB:
                    dve.wait_ge(ffn_added, g + 1)
                dve.wait_ge(yd_loaded[g % 2], 16 * TOP * (g // 2 + 1))
                dve.tensor_tensor(xv, xv, yd[:, g % 2, 0], ALU.add).then_inc(yd_link, 1)
                dve.wait_ge(yd_link, g + 1)
                dve.tensor_tensor(xv, xv, yd[:, g % 2, 1], ALU.add).then_inc(fin_ready, 1)

            def finish_ready():
                if done[0] < NGB:
                    finish()

            shared(NGB // 2, False, finish_ready)
            for _ in range(NG):
                finish()

        @block.tensor
        def _(pe):
            def mm(o, a, b, first, last, check=False):
                return pe.matmul(o, a, b, start=first, stop=last, skip_group_check=not check)

            pe.wait_ge(kv_loaded, 16 * N_KV)
            pe.wait_ge(const_ready, N_CONST)
            for hf in range(HF):
                mm(bank[hf][:, 0:BK], wk_a[:, bass.ts(hf, P)], ctx_a, True, False)
                mm(bank[hf][:, 0:BK], wk_b[:, bass.ts(hf, P)], ctx_b, False, True).then_inc(k_ready, 1)
            for b in range(B):
                o = bank[2 + b][:, 0:C]
                mm(o, ctx2_a[:, b].rearrange("p a k -> p (a k)"), wv_a, True, False)
                mm(o, ctx2_b[:, b].rearrange("p a k -> p (a k)"), wv_b, False, False)
                mm(o, ones_r, bv_r, False, True).then_inc(v_ready, 1)
            mm(bank[6][:, 0:C], ones_r, bo_r, True, True).then_inc(bo_ready, 1)
            pe.wait_ge(proj_split, 3)
            pe.wait_ge(kblk_ready, 2 * B * HF)
            pe.wait_ge(v_copied, B)
            pe.wait_ge(bo_copied, 1)

            THREE = ((0, 0), (0, 1), (1, 0))

            def row_scores(b, n, s):
                for i in range(GT):
                    for hf in range(HF):
                        pe.wait_ge(qh_ready, HF * n + hf + 1)
                        if not (isinstance(n, int) and n == 0 and i == 0):
                            pe.wait_ge(smax_used, HF * (GT * n + i) + hf - 1)
                        mm(bank[4 + hf][:, :], qx[:, 0, hf, bass.ts(GT * n + i, P)],
                           k_blk[:, 0, bass.ds(b, 1), hf].rearrange("p a h k -> p (a h k)"),
                           True, True).then_inc(smax_ready, 1)

            def max_t(n, s):
                pe.wait_ge(mcl_ready, n + 1)
                if not (isinstance(n, int) and n == 0):
                    pe.wait_ge(mt_copied, n)
                for i in range(GT):
                    ins = pe.transpose(bank[6][0:HD, 64 * i:64 * i + 64].bitcast(F16), m_cl[:, s, i], ident[:, :])
                ins.then_inc(mt_ready, 1)

            def phase1(b):
                loop = not isinstance(b, int)
                for s in range(2):
                    n = 2 * b + s
                    if loop or s == 1:
                        row_scores(b if s == 1 else b - 1, n - 1, 1 - s)
                    pe.wait_ge(xnl_ready, n + 1)
                    for i in range(GT):
                        if loop or s > 0 or i > 1:
                            pe.wait_ge(xt_copied, GT * n + i - 1)
                        for sp_ in range(2):
                            src = (xn_h, xn_l)[sp_]
                            for hf in range(HF):
                                c = (sp_ * HF + hf) * 64
                                ins = pe.transpose(bank[i % 2][:, c:c + 64].bitcast(F16),
                                                   src[:, s, i, bass.ts(hf, P)], ident[:, :])
                        ins.then_inc(xt_ready, 1)
                    pe.wait_ge(xt_copied, GT * (n + 1))
                    for hf in range(HF):
                        if loop or s > 0:
                            pe.wait_ge(qf_ready, HF * (n - 1) + hf + 1)
                        for i, (a, c) in enumerate(THREE):
                            for cc in range(HF):
                                ins = mm(bank[2 + hf][:, :], wq_hl[:, a, cc, bass.ts(hf, P)], xn_t[:, s, c, cc],
                                         i == 0 and cc == 0, i == 2 and cc == HF - 1)
                        ins.then_inc(q_ready, 1)
                    if loop or s == 1:
                        max_t(n - 1, 1 - s)

            batches(pe, phase1)
            row_scores(B - 1, NG - 1, 1)
            pe.wait_ge(qf_ready, NG * HF)
            mm(bank[7][:, 0:HF * NG + HF], ones_f, q_sum, True, True).then_inc(flag_ready, 1)
            max_t(NG - 1, 1)
            pe.wait_ge(mt_copied, NG)
            pe.wait_ge(ql_ready, NG * HF)
            pe.wait_ge(vblk_ready, 4)
            pe.wait_ge(scale_ready, 1)

            def scores(u, b, jp):
                k = JP * u + jp
                if not isinstance(u, int) or u > 0:
                    pe.wait_ge(exp_ready, k - 3)
                for j2 in range(2):
                    j = 2 * jp + j2
                    hf, r = divmod(j, HH // 2)
                    for i, (a, c) in enumerate(THREE):
                        ins = mm(bank[jp][:, bass.ts(j2, UC)],
                                 k_blk[:, a, bass.ds(b, 1), hf, 2 * r:2 * r + 2, :].rearrange("p a h k -> p (a h k)"),
                                 qx[:, c, hf, bass.ts(u, UC)], j2 == 0 and i == 0, False)
                ins.then_inc(st_scored, 1)

            def subtract_max(u, jp):
                k = JP * u + jp
                pe.wait_ge(st_clipped, k + 1)
                for j2 in range(2):
                    ins = mm(bank[jp][:, bass.ts(j2, UC)],
                             neg_ind[:, 2 * jp + j2].rearrange("p a k -> p (a k)"),
                             m_t[:, bass.ts(u, UC)], False, True)
                ins.then_inc(st_ready, 1)

            def weigh(u, b, jp):
                k = JP * u + jp
                pe.wait_ge(pl_ready, k + 1)
                if jp == 0 and (not isinstance(u, int) or u > 0):
                    pe.wait_ge(of_ready, u)
                for j2 in range(2):
                    j = 2 * jp + j2
                    for t in range(UT):
                        c = bass.ds(j2 * UC + t * P, P)
                        vh = v_blk_h[:, bass.ds(b, 1), j, :].squeeze(1)
                        vl = v_blk_l[:, bass.ds(b, 1), j, :].squeeze(1)
                        mm(bank[4 + t][:, j * OW:j * OW + OW], p_h[:, jp, c], vh, j == 0, False)
                        mm(bank[4 + t][:, j * OW:j * OW + OW], p_l[:, jp, c], vh, False, False)
                        ins = mm(bank[4 + t][:, j * OW:j * OW + 2 * D], p_h[:, jp, c], vl, False, True)
                ins.then_inc(pv_ready, 1)

            def step_of(k_u, jp, back):
                if jp >= back:
                    return k_u, jp - back
                return k_u - 1, jp - back + JP

            def unit(u, s, b, b_prev):
                for jp in range(JP):
                    if known(u, 0):
                        scores(u, b, jp)
                    v, q = step_of(u, jp, 1)
                    if known(v, 0):
                        subtract_max(v, q)
                    v, q = step_of(u, jp, 3)
                    if known(v, 0):
                        weigh(v, b if jp >= 3 else b_prev, q)
                    if jp == 0 and known(u, 5):
                        pe.wait_ge(x2l_ready, u - 4)
                        if known(u, 3):
                            pe.wait_ge(ot_copied, u - 2)
                        else:
                            pe.wait_ge(x2t_copied, u - 5)
                        for t in range(UT):
                            for sp_ in range(2):
                                for hf in range(HF):
                                    c = ((t * 2 + sp_) * HF + hf) * 64
                                    ins = pe.transpose(bank[6][:, c:c + 64].bitcast(F16),
                                                       (x2_h, x2_l)[sp_][:, (s + 1) % 2, t, bass.ts(hf, P)],
                                                       ident[:, :])
                        ins.then_inc(x2t_ready, 1)
                    if jp == 0 and known(u, 3):
                        pe.wait_ge(ot_copied, u - 2)
                        if old(u, 6):
                            pe.wait_ge(lg_copied, u - 5)
                        for t in range(UT):
                            for i, (a, c) in enumerate(THREE):
                                for hf in range(HF):
                                    ins = mm(bank[7][:, bass.ts(t, C)], o_t[:, (s + 1) % 2, t, c, hf], wo_hl[:, a, hf],
                                             t == 0 and i == 0 and hf == 0, i == 2 and hf == HF - 1)
                        ins.then_inc(y_ready, 1)
                    if jp == 2 and known(u, 2):
                        pe.wait_ge(ol_ready, u - 1)
                        if known(u, 5):
                            pe.wait_ge(x2t_copied, u - 4)
                        elif old(u, 3):
                            pe.wait_ge(ot_copied, u - 2)
                        for t in range(UT):
                            for sp_ in range(2):
                                for hf in range(HF):
                                    c = ((t * 2 + sp_) * HF + hf) * 64
                                    ins = pe.transpose(bank[6][:, c:c + 64].bitcast(F16),
                                                       (o_h, o_l)[sp_][:, s % 2, t, bass.ts(hf, P)], ident[:, :])
                        ins.then_inc(ot_ready, 1)
                    if jp == 2 and known(u, 5):
                        pe.wait_ge(x2t_copied, u - 4)
                        if known(u, 3):
                            pe.wait_ge(y_added, u - 2)
                        else:
                            pe.wait_ge(lg_copied, u - 5)
                        for t in range(UT):
                            for i, (a, c) in enumerate(THREE + ((1, 1),)):
                                for hf in range(HF):
                                    ins = mm(bank[7][:, bass.ts(t, E)], qx[:, c, hf, bass.ts(UT * (u - 5) + t, P)],
                                             gate_hl[:, a, hf, :], t == 0 and i == 0 and hf == 0,
                                             i == 3 and hf == HF - 1)
                        ins.then_inc(lg_ready, 1)

            for u in range(2 * UB):
                unit(u, u % UB, u // UB, (u - 1) // UB if u else 0)
            with pe.Fori(2, B) as b:
                for s in range(UB):
                    unit(UB * b + s, s, b, b if s > 0 else b - 1)
            for s in range(LAST_LAG):
                unit(NU + s, s % UB, B, B - 1)

            pe.wait_ge(pick_ready, 1)
            a_et = pick_et.rearrange("p e t -> p (e t)")
            mm(bank[7][:, 0:E * NT], tri[:, :], a_et, True, True)
            mm(bank[7][:, E * NT:2 * E * NT], ones_h[:, :], a_et, False, True).then_inc(count_ready, 1)

            def up(n, hc):
                k = FC * n + hc
                if not (isinstance(k, int) and k < 2):
                    pe.wait_ge(hf_ready, k - 1)
                for m in range(2):
                    for i, (a, c) in enumerate(THREE):
                        for hf in range(HF):
                            ins = mm(bank[2 * m + hc % 2][:, :],
                                     w_sh[:, m, a, hf * F + hc * P:hf * F + hc * P + P],
                                     qx[:, c, hf, bass.ts(n, GC)],
                                     i == 0 and hf == 0, i == 2 and hf == HF - 1)
                ins.then_inc(gu_ready, 1)

            def down(n, s, hc):
                k = FC * n + hc
                pe.wait_ge(hl_ready, k + 1)
                if hc == 0 and not (isinstance(n, int) and n < 2):
                    pe.wait_ge(ffn_added, n - 1)
                for t in range(GT):
                    o = bank[4 + 2 * s + t // 2][:, bass.ts(t % 2, C)]
                    for i, (a, c) in enumerate(THREE):
                        ins = mm(o, (h_h, h_l)[c][:, hc % 2, bass.ts(t, P)], w_sh[:, 2, a, bass.ts(hc, C)],
                                 hc == 0 and i == 0 and t % 2 == 0, hc == FC - 1 and i == 2)
                ins.then_inc(down_used, 1)

            def shared(gp):
                for s in range(2):
                    n = 2 * gp + s
                    up(n, 0)
                    for hc in range(1, FC):
                        up(n, hc)
                        down(n, s, hc - 1)
                    down(n, s, FC - 1)

            pe.wait_ge(w_lo, 3)
            pe.wait_ge(place_ready, 1)
            shared(0)
            with pe.Fori(1, NGB // 2) as gp:
                shared(gp)

            pe.wait_ge(w_lo, 3 * (E + 1))
            pe.wait_ge(ffn_added, NGB)

            expert = {}

            def slot(it, s):
                i = 8 * it + s
                if has(i, 0):
                    apart(pe, sp_xt_copied, i + 1, place_ready, 1)
                    if old(i, 2):
                        pe.wait_ge(sp_h, i - 1)
                    e = pe.value_load(slot_e[0:1, bass.ds(i, 1)], min_val=0, max_val=E - 1)
                    for m in range(2):
                        for j, (a, c) in enumerate(THREE):
                            for hf in range(HF):
                                ins = mm(bank[2 * m + s % 2][:, :], xgt[:, s % 2, c, hf],
                                         w_rt[:, bass.ds(e, 1), m, a, bass.ts(hf, F)].squeeze(1),
                                         j == 0 and hf == 0, j == 2 and hf == HF - 1)
                    ins.then_inc(sp_up, 1)
                if has(i, 1):
                    r = (s + 1) % 4
                    pe.wait_ge(x_got[r], 16 * (2 * it + (s + 1) // 4 + 1))
                    if has(i, 0):
                        pe.wait_ge(sp_xt_copied, i + 1)
                    for sp_ in range(2):
                        for hf in range(HF):
                            c = (sp_ * HF + hf)
                            ins = pe.transpose(bank[4][:, 64 * c:64 * c + 64].bitcast(F16),
                                               xg[:, r, bass.ts(c, P)], ident[:, :])
                    ins.then_inc(sp_xt, 1)
                if has(i, -2):
                    apart(pe, sp_ht_copied, i - 1, place_ready, 1)
                    if old(i, 4):
                        pe.wait_ge(sp_y, i - 3)
                    e = pe.value_load(slot_e[0:1, bass.ds(i - 2, 1)], min_val=0, max_val=E - 1)
                    for j, (a, c) in enumerate(THREE):
                        for f in range(FC):
                            ins = mm(bank[6 + s % 2][:, 0:C], ht[:, s % 2, c, f],
                                     w_rt[:, bass.ds(e, 1), 2, a, bass.ts(f, C)].squeeze(1),
                                     j == 0 and f == 0, j == 2 and f == FC - 1)
                    ins.then_inc(sp_down, 1)
                if has(i, -1):
                    pe.wait_ge(sp_hl, i)
                    if old(i, 2):
                        pe.wait_ge(sp_ht_copied, i - 1)
                    for sp_ in range(2):
                        for f in range(FC):
                            c = (sp_ * FC + f) * 64
                            ins = pe.transpose(bank[5][:, c:c + 64].bitcast(F16),
                                               (h_h, h_l)[sp_][:, (s + 1) % 2, bass.ts(f, P)], ident[:, :])
                    ins.then_inc(sp_ht, 1)

            run_slots(pe, slot)
            pe.wait_ge(sp_y, NS)
            shared(NGB // 2)


def kernel(**inputs):
    import numpy as np
    import concourse.bacc as bacc
    from concourse import mybir as mb
    from concourse.bass_utils import run_bass_kernel_spmd as run

    a = {k: np.asarray(v) for k, v in inputs.items()}

    def rows(w):
        *lead, k, n = w.shape
        return np.swapaxes(w.reshape(*lead, k // 128, 128, n), -3, -2).reshape(*lead, 128, k // 128 * n)

    arrays = {
        'x': a['x'],
        'ctx_t': a['ctx_768'].transpose(2, 0, 1).reshape(a['ctx_768'].shape[2], -1),
        'wq': a['L0_xattn_Wq'], 'bq': a['L0_xattn_bq'].reshape(-1, 128).T, 'wk': a['L0_xattn_Wk'], 'bk': a['L0_xattn_bk'].reshape(-1, 128).T,
        'wv': a['L0_xattn_Wv'], 'bv': a['L0_xattn_bv'], 'wo': a['L0_xattn_Wo'], 'bo': a['L0_xattn_bo'],
        'gate_t': a['L0_ffn_gate_w'].T,
        'w_all': np.concatenate([
            np.stack([rows(a[f'L0_ffn_sh_{m}'].T) for m in ('gate', 'up', 'down')]),
            np.stack([rows(a[f'L0_ffn_{m}'].transpose(0, 2, 1)) for m in ('eg', 'eu', 'ed')],
                     axis=1).reshape(-1, 128, a['L0_ffn_sh_gate'].shape[0] * 2)]),
    }
    arrays = {k: np.ascontiguousarray(v) for k, v in arrays.items()}
    nc = bacc.Bacc("TRN2", target_bir_lowering=False, num_devices=1)
    aps = [nc.dram_tensor(f"in_{k}", v.shape, mb.dt.from_np(v.dtype), kind="ExternalInput").ap()
           for k, v in arrays.items()]
    out = nc.dram_tensor("out_0", a['x'].shape, mb.dt.float32, kind="ExternalOutput").ap()
    build(nc, *aps, out)
    r = run(nc, [{f"in_{k}": v for k, v in arrays.items()}], core_ids=[0])
    return r.results[0]["out_0"]
```
